# Optimizing a Trainium2 kernel written in Bass

```python
import numpy as np
import jax
import jax.numpy as jnp

def _softmax(x, axis=-1):
    return jax.nn.softmax(x, axis=axis)
def _gelu(x):
    return jax.nn.gelu(x, approximate=True)
def _silu(x):
    return jax.nn.silu(x)
def _sigmoid(x):
    return jax.nn.sigmoid(x)
def _layernorm(x, axis=-1, eps=1e-5):
    m = jnp.mean(x, axis=axis, keepdims=True)
    v = jnp.var(x, axis=axis, keepdims=True)
    return (x - m) / jnp.sqrt(v + eps)
def _scatter_add(tgt, idx, src, axis=0):
    return tgt.at[idx].add(src)
def _segment_sum(src, seg, n):
    return jax.ops.segment_sum(src, seg, n)

kernel_name = 'mk_adj_resnorm_d4_adj_256_71fc2b'

def setup_inputs(seed: int = 0):
    np.random.seed(seed)
    _w = jnp.asarray
    def _rec_inputs():
        import jax
        import jax.numpy as jnp
        _gk = jax.random.key(seed)
        x = -0.0002928 + 1 * jax.random.normal(jax.random.fold_in(_gk, 1), (32, 512, 256), jnp.float32)
        _w = (1.0 + jnp.arange(512, dtype=jnp.float32)) ** -0.5
        _w = _w / _w.mean()
        _pij = jnp.clip(0.03125 * _w[:, None] * _w[None, :], 0.0, 1.0)
        _a = jax.random.uniform(jax.random.fold_in(_gk, 2), (32, 512, 512)) < _pij
        _a = jnp.logical_or(_a, jnp.swapaxes(_a, -1, -2))
        _a = jnp.logical_or(_a, jnp.eye(512, dtype=bool))
        _af = _a.astype(jnp.float32)
        _af = _af * jax.random.uniform(jax.random.fold_in(_gk, 3), (32, 512, 512), jnp.float32, 0.05, 1)
        adj = _af
        return x, adj
    x, adj = _rec_inputs()
    def _L0_gnn_setup():
        import jax, jax.numpy as jnp
        import numpy as np
        B, N, D, H = (8, 2048, 256, 1024)
        RMS_EPS = 1e-06

        def _rmsnorm(h, w, eps=RMS_EPS):
            var = jnp.mean(jnp.square(h), axis=-1, keepdims=True)
            return h * jax.lax.rsqrt(var + eps) * w
        key = jax.random.key(seed)
        ks = jax.random.split(key, 5)
        x = jax.random.normal(ks[0], (B, N, D), dtype=jnp.float32)
        adjacency = jax.random.uniform(ks[1], (B, N, N), dtype=jnp.float32)
        epsilon = jnp.zeros((), dtype=jnp.float32)
        W1 = jax.random.normal(ks[2], (D, H), dtype=jnp.float32) * (1.0 / np.sqrt(D))
        b1 = jnp.zeros((H,), dtype=jnp.float32)
        rms_weight = jnp.ones((H,), dtype=jnp.float32)
        W2 = jax.random.normal(ks[3], (H, D), dtype=jnp.float32) * (1.0 / np.sqrt(H))
        b2 = jnp.zeros((D,), dtype=jnp.float32)
        return {'x': x, 'adjacency': adjacency, 'epsilon': epsilon, 'W1': W1, 'b1': b1, 'rms_weight': rms_weight, 'W2': W2, 'b2': b2}
    _L0_gnn_all = _L0_gnn_setup()
    _L0_gnn_in = {k: v for k, v in _L0_gnn_all.items() if k in ('epsilon', 'W1', 'b1', 'rms_weight', 'W2', 'b2', )}
    del _L0_gnn_all

    def _L1_gnn_setup():
        import jax, jax.numpy as jnp
        import numpy as np
        IN_DIM = 256
        OUT_DIM = 256
        key = jax.random.key(seed)
        k1, k2, k3, k4 = jax.random.split(key, 4)
        B, N = (8, 2048)
        X = jax.random.normal(k1, (B, N, IN_DIM), dtype=jnp.float32)
        adj = jax.random.uniform(k2, (B, N, N), dtype=jnp.float32)
        bound = 1.0 / np.sqrt(IN_DIM)
        W = jax.random.uniform(k3, (OUT_DIM, IN_DIM), minval=-bound, maxval=bound, dtype=jnp.float32)
        b = jax.random.uniform(k4, (OUT_DIM,), minval=-bound, maxval=bound, dtype=jnp.float32)
        return {'X': X, 'adj': adj, 'W': W, 'b': b}
    _L1_gnn_all = _L1_gnn_setup()
    _L1_gnn_in = {k: v for k, v in _L1_gnn_all.items() if k in ('W', 'b', )}
    del _L1_gnn_all

    def _L2_gnn_setup():
        import jax, jax.numpy as jnp
        import numpy as np
        key = jax.random.key(seed)
        k1, k2, k3 = jax.random.split(key, 3)
        b, n, d, f = (16, 2048, 256, 256)
        features = jax.random.normal(k1, (b, n, d), dtype=jnp.float32)
        A = jax.random.uniform(k2, (b, n, n), dtype=jnp.float32)
        A = A / jnp.sum(A, axis=-1, keepdims=True)
        weight = jax.random.normal(k3, (2 * d, f), dtype=jnp.float32) * (1.0 / np.sqrt(2 * d))
        bias = jnp.zeros((f,), dtype=jnp.float32)
        return {'features': features, 'A': A, 'weight': weight, 'bias': bias}
    _L2_gnn_all = _L2_gnn_setup()
    _L2_gnn_in = {k: v for k, v in _L2_gnn_all.items() if k in ('weight', 'bias', )}
    del _L2_gnn_all

    def _L3_gnn_setup():
        import jax, jax.numpy as jnp
        import numpy as np
        B, N, D = (8, 512, 256)
        key = jax.random.key(seed)
        ks = jax.random.split(key, 10)
        s = 1.0 / np.sqrt(D)
        u = lambda k, shape: jax.random.uniform(k, shape, jnp.float32, -s, s)
        return {'h_e': jax.random.normal(ks[0], (B, N, D), jnp.float32), 'adj': jax.random.uniform(ks[1], (B, N, N), jnp.float32), 'W_ioux': u(ks[2], (2 * D, D)), 'b_ioux': u(ks[3], (2 * D,)), 'W_iouh': u(ks[4], (2 * D, D)), 'b_iouh': u(ks[5], (2 * D,)), 'W_coux': u(ks[6], (D, D)), 'b_coux': u(ks[7], (D,)), 'W_couh': u(ks[8], (D, D)), 'b_couh': u(ks[9], (D,))}
    _L3_gnn_all = _L3_gnn_setup()
    _L3_gnn_in = {k: v for k, v in _L3_gnn_all.items() if k in ('W_ioux', 'b_ioux', 'W_iouh', 'b_iouh', 'W_coux', 'b_coux', 'W_couh', 'b_couh', )}
    del _L3_gnn_all

    return {
        "x": x,
        "adj": adj,
        "L0_gnn_epsilon": _L0_gnn_in["epsilon"],
        "L0_gnn_W1": _L0_gnn_in["W1"],
        "L0_gnn_b1": _L0_gnn_in["b1"],
        "L0_gnn_rms_weight": _L0_gnn_in["rms_weight"],
        "L0_gnn_W2": _L0_gnn_in["W2"],
        "L0_gnn_b2": _L0_gnn_in["b2"],
        "L1_gnn_W": _L1_gnn_in["W"],
        "L1_gnn_b": _L1_gnn_in["b"],
        "L2_gnn_weight": _L2_gnn_in["weight"],
        "L2_gnn_bias": _L2_gnn_in["bias"],
        "L3_gnn_W_ioux": _L3_gnn_in["W_ioux"],
        "L3_gnn_b_ioux": _L3_gnn_in["b_ioux"],
        "L3_gnn_W_iouh": _L3_gnn_in["W_iouh"],
        "L3_gnn_b_iouh": _L3_gnn_in["b_iouh"],
        "L3_gnn_W_coux": _L3_gnn_in["W_coux"],
        "L3_gnn_b_coux": _L3_gnn_in["b_coux"],
        "L3_gnn_W_couh": _L3_gnn_in["W_couh"],
        "L3_gnn_b_couh": _L3_gnn_in["b_couh"],
    }

def reference(x, adj, L0_gnn_epsilon, L0_gnn_W1, L0_gnn_b1, L0_gnn_rms_weight, L0_gnn_W2, L0_gnn_b2, L1_gnn_W, L1_gnn_b, L2_gnn_weight, L2_gnn_bias, L3_gnn_W_ioux, L3_gnn_b_ioux, L3_gnn_W_iouh, L3_gnn_b_iouh, L3_gnn_W_coux, L3_gnn_b_coux, L3_gnn_W_couh, L3_gnn_b_couh):
    import jax
    import jax.numpy as jnp
    def _L0_gnn_ref(x, adjacency, epsilon, W1, b1, rms_weight, W2, b2):
        import jax, jax.numpy as jnp
        import numpy as np
        B, N, D, H = (8, 2048, 256, 1024)
        RMS_EPS = 1e-06

        def _rmsnorm(h, w, eps=RMS_EPS):
            var = jnp.mean(jnp.square(h), axis=-1, keepdims=True)
            return h * jax.lax.rsqrt(var + eps) * w
        neighbor_sum = jnp.einsum('bnm,bmd->bnd', adjacency, x)
        agg = epsilon * x + neighbor_sum
        h = jnp.einsum('bnd,dh->bnh', agg, W1) + b1
        h = jax.nn.silu(_rmsnorm(h, rms_weight))
        out = jnp.einsum('bnh,hd->bnd', h, W2) + b2
        return out

    def _L1_gnn_ref(X, adj, W, b):
        import jax, jax.numpy as jnp
        import numpy as np
        IN_DIM = 256
        OUT_DIM = 256
        N = adj.shape[-1]
        adj_hat = adj + jnp.eye(N, dtype=adj.dtype)
        d = jnp.sum(adj_hat, axis=-1) ** (-0.5)
        adj_norm = d[..., :, None] * adj_hat * d[..., None, :]
        H = jnp.matmul(adj_norm, X)
        out = jnp.einsum('bnf,of->bno', H, W) + b
        return jax.nn.relu(out)

    def _L2_gnn_ref(features, A, weight, bias):
        import jax, jax.numpy as jnp
        import numpy as np
        agg = jnp.einsum('bnm,bmd->bnd', A, features)
        d = features.shape[-1]
        out = jnp.einsum('bnd,df->bnf', features, weight[:d]) + jnp.einsum('bnd,df->bnf', agg, weight[d:]) + bias
        return jax.nn.relu(out)

    def _L3_gnn_ref(h_e, adj, W_ioux, b_ioux, W_iouh, b_iouh, W_coux, b_coux, W_couh, b_couh):
        import jax, jax.numpy as jnp
        import numpy as np
        B, N, D = (8, 512, 256)
        n = h_e.shape[1]
        d = jnp.sum(adj, axis=-1)
        dinv = jnp.where(d != 0, 1.0 / jnp.where(d != 0, d, 1.0), 0.0)
        norm_adjT = jnp.swapaxes(adj, 1, 2) * dinv[:, :, None]

        def step(h, i):
            x = jnp.take(h_e, i, axis=1)
            row = jnp.take(norm_adjT, i, axis=1)
            x_par = jnp.einsum('bj,bjd->bd', row, h)
            iou = x @ W_ioux.T + b_ioux + x_par @ W_iouh.T + b_iouh
            r, z = jnp.split(iou, 2, axis=1)
            r, z = (jax.nn.sigmoid(r), jax.nn.sigmoid(z))
            hc = jnp.tanh(x @ W_coux.T + b_coux + x_par * r @ W_couh.T + b_couh)
            h_new = z * x_par + (1.0 - z) * hc
            h = jax.lax.dynamic_update_slice(h, h_new[:, None, :], (0, i, 0))
            return (h, None)
        h_out, _ = jax.lax.scan(step, h_e, jnp.arange(n))
        return h_out

    x = _layernorm(x + _L0_gnn_ref(x, adj, L0_gnn_epsilon, L0_gnn_W1, L0_gnn_b1, L0_gnn_rms_weight, L0_gnn_W2, L0_gnn_b2), axis=-1)
    x = _layernorm(x + _L1_gnn_ref(x, adj, L1_gnn_W, L1_gnn_b), axis=-1)
    x = _layernorm(x + _L2_gnn_ref(x, adj, L2_gnn_weight, L2_gnn_bias), axis=-1)
    x = _layernorm(x + _L3_gnn_ref(x, adj, L3_gnn_W_ioux, L3_gnn_b_ioux, L3_gnn_W_iouh, L3_gnn_b_iouh, L3_gnn_W_coux, L3_gnn_b_coux, L3_gnn_W_couh, L3_gnn_b_couh), axis=-1)
    return x


_drawn_inputs = setup_inputs


def setup_inputs(seed=0):
    import zlib

    import numpy as np

    out = dict(_drawn_inputs(seed))
    spreads = {'L0_gnn_b1': (0.0, 0.1),
     'L0_gnn_rms_weight': (1.0, 0.2),
     'L0_gnn_b2': (0.0, 0.1),
     'L2_gnn_bias': (0.0, 0.1)}
    factors = {'L3_gnn_b_ioux': 8.0, 'L3_gnn_b_iouh': 8.0, 'L3_gnn_b_coux': 3.302, 'L3_gnn_b_couh': 3.317}
    for name, (base, spread) in spreads.items():
        noise = np.random.default_rng([zlib.crc32(name.encode()), seed]).standard_normal(out[name].shape)
        drawn = base * np.exp(spread * noise) if base else spread * noise
        out[name] = jnp.asarray(drawn.astype(out[name].dtype))
    for name, factor in factors.items():
        out[name] = (out[name] * factor).astype(out[name].dtype)
    return out
```

```python
from contextlib import ExitStack

import concourse.bass as bass
from concourse import mybir

ALU = mybir.AluOpType
ACT = mybir.ActivationFunctionType
F32 = mybir.dt.float32
AX_X = mybir.AxisListType.X

P = 128
LN_EPS = 1e-5
RMS_EPS = 1e-6


def diagonal(t, n, width):
    whole = t[:, :, :]
    return bass.AP(tensor=whole.tensor, offset=whole.offset,
                   ap=[whole.ap[0], [width + P, n], [1, P]])


def graph_layers(nc, x, adj, eps, W1, b1, rmsw, W2, b2, W_gcn, b_gcn, W_sage, b_sage,
                 x3, x3T, dinv):
    NB, N, D = x.shape
    H = W1.shape[1]
    NT, DC, HC = N // P, D // P, H // P
    BLK = x3T.shape[4]
    SUB = dinv.shape[2]
    NBLK = N // BLK
    PAIRS = NB // 2

    with ExitStack() as ctx:
        def sb(name, shape, dt=F32):
            return ctx.enter_context(nc.sbuf_tensor(name, shape, dt))

        def sem(name):
            return ctx.enter_context(nc.semaphore(name))

        w1 = sb("w1", [P, DC, H])
        w2 = sb("w2", [P, HC, D])
        wg = sb("wg", [P, DC, D])
        ws = sb("ws", [P, 2 * DC, D])
        b1r = sb("b1r", [P, H])
        rmsr = sb("rmsr", [P, H])
        b2r = sb("b2r", [P, D])
        bgr = sb("bgr", [P, D])
        bsr = sb("bsr", [P, D])
        epsc = sb("epsc", [P, 1])
        ident = sb("ident", [P, P])
        eident = sb("eident", [P, P])
        mhalf = sb("mhalf", [P, NT])
        rs_all = sb("rs_all", [P, NT, NB])
        rsT = sb("rsT", [P, P])
        zero = sb("zero", [P, P])
        nonzero = sb("nonzero", [P, P])
        safe = sb("safe", [P, P])

        adj_in = [sb(f"adj_in{s}", [P, NT, N]) for s in range(2)]
        x_in = [sb(f"x_in{s}", [P, NT, D]) for s in range(2)]
        adjT = [sb(f"adjT{s}", [P, NT, N]) for s in range(2)]
        dsave = [sb(f"dsave{s}", [P, NT, P]) for s in range(2)]
        xa = [sb(f"xa{s}", [P, NT, D]) for s in range(2)]
        xs = [sb(f"xs{s}", [P, NT, D]) for s in range(2)]
        agg = [sb(f"agg{s}", [P, DC, N]) for s in range(2)]
        xT = [sb(f"xT{s}", [P, DC, N]) for s in range(2)]
        x3Tb = [sb(f"x3Tb{s}", [P, DC, N]) for s in range(2)]
        hb = [sb(f"hb{k}", [P, H]) for k in range(2)]
        hT = [sb(f"hT{k}", [P, HC, P]) for k in range(2)]
        sqj = sb("sqj", [P, H])
        tmp = sb("tmp", [P, 2, D])
        ss = sb("ss", [P, 2])
        rr = sb("rr", [P, 2])
        rr2 = sb("rr2", [P, 2])
        stats = sb("stats", [P, NT, 6])
        mv = sb("mv", [P, 2, NT, 2])
        ve = sb("ve", [P, 2, NT])
        rstd = sb("rstd", [P, 2, NT])
        rs = sb("rs", [P, 2, NT])
        rs1 = sb("rs1", [P, 2, NT])
        dg = sb("dg", [P, 2, NT])

        T = [ctx.enter_context(nc.psum_tensor(f"T{k}", [P, 512], F32)) for k in range(2)]
        G = [ctx.enter_context(nc.psum_tensor(f"G{k}", [P, 512], F32)) for k in range(2)]
        HP = [ctx.enter_context(nc.psum_tensor(f"HP{k}", [P, 512], F32)) for k in range(2)]
        O = [ctx.enter_context(nc.psum_tensor(f"O{k}", [P, 512], F32)) for k in range(2)]

        w_ld = sem("w_ld")
        ld_adj = [sem(f"ld_adj{s}") for s in range(2)]
        ld_x = [sem(f"ld_x{s}") for s in range(2)]
        out_x = [sem(f"out_x{s}") for s in range(2)]
        out_T = [sem(f"out_T{s}") for s in range(2)]
        out_rs = sem("out_rs")
        setup = sem("setup")
        t_full, t_evac = sem("t_full"), sem("t_evac")
        g_full, g_evac = sem("g_full"), sem("g_evac")
        h_full, h_evac = sem("h_full"), sem("h_evac")
        o_full, o_evac = sem("o_full"), sem("o_evac")
        sq_done, r_done, y_done = sem("sq_done"), sem("r_done"), sem("y_done")
        mv_done, rstd_done, x_done, xs_done = sem("mv_done"), sem("rstd_done"), sem("x_done"), sem("xs_done")
        rs_done, dg_done = sem("rs_done"), sem("dg_done")
        dia_done = sem("dia_done")
        rsT_full = sem("rsT_full")
        pool_gate, dve_gate, sp_gate = sem("pool_gate"), sem("dve_gate"), sem("sp_gate1")
        v_step, p_step = sem("v_step"), sem("p_step")

        TG, GG, HG, OG = 32, 12, 16, 24
        AT0, AT1, Y0, Y1, XT0, XT1, XF0, XF1 = 0, 4, 8, 16, 24, 26, 28, 30
        TADJ, TY, TX, TF = (AT0, AT1), (Y0, Y1), (XT0, XT1), (XF0, XF1)
        AGG = ((0, 2), (4, 6), (8, 10))
        VPER, PPER = 86, 18

        block = ctx.enter_context(nc.Block())

        @block.sync
        def _(sp):
            for dst, src in ((w1, W1.rearrange("(c p) h -> p c h", p=P)), (w2, W2.rearrange("(c p) d -> p c d", p=P)),
                             (wg, W_gcn.rearrange("(c p) d -> p c d", p=P)),
                             (ws, W_sage.rearrange("(c p) d -> p c d", p=P))):
                sp.dma_start(dst[:], src).then_inc(w_ld, 16)
            for dst, src in ((b1r, b1), (rmsr, rmsw), (b2r, b2), (bgr, b_gcn), (bsr, b_sage), (epsc, eps)):
                sp.dma_start(dst[:], src.partition_broadcast(P)).then_inc(w_ld, 16)

            def load(b, s):
                sp.dma_start(adj_in[s][:], adj[b].rearrange("(t p) m -> p t m", p=P)).then_inc(ld_adj[s], 16)
                sp.dma_start(x_in[s][:], x[b].rearrange("(t p) d -> p t d", p=P)).then_inc(ld_x[s], 16)

            def store(it, b, s):
                sp.wait_ge(x_done, it * 6 + 5 + s)
                sp.sem_inc(sp_gate, 1)
                sp.dma_start(x3[b].rearrange("(t p) d -> p t d", p=P), xa[s][:]).then_inc(out_x[s], 16)
                sp.wait_ge(t_evac, it * TG + TF[s] + 2 + 2)
                sp.sem_inc(sp_gate, 1)
                for c in range(DC):
                    sp.dma_start(x3T[:, :, c, b, :].rearrange("k p i -> p k i"),
                                 x3Tb[s][:, c, :].rearrange("p (k i) -> p k i", i=BLK)).then_inc(out_T[s], 16)

            for s in range(2):
                load(s, s)
            if PAIRS > 1:
                with sp.Fori(0, PAIRS - 1) as it:
                    for s in range(2):
                        sp.wait_ge(t_full, it * TG + TADJ[s] + 4)
                        sp.sem_inc(sp_gate, 1)
                        sp.sem_inc(sp_gate, 1)
                        sp.wait_ge(rs_done, it * 2 + s + 1)
                        sp.sem_inc(sp_gate, 1)
                        sp.wait_ge(g_full, it * GG + AGG[0][s] + 2)
                        sp.sem_inc(sp_gate, 1)
                        sp.wait_ge(o_evac, it * OG + 4 * s + 4 + 2)
                        sp.sem_inc(sp_gate, 1)
                        load(2 * it + 2 + s, s)
                    for s in range(2):
                        store(it, 2 * it + s, s)
            for s in range(2):
                store(PAIRS - 1, NB - 2 + s, s)
            sp.wait_ge(rsT_full, 6)
            for t in range(NT):
                sp.dma_start(dinv[t * P // SUB:(t + 1) * P // SUB].rearrange("u b q -> b u q"),
                             rsT[t * NB:(t + 1) * NB, :].rearrange("b (u q) -> b u q", q=SUB)).then_inc(out_rs, 16)
            for s in range(2):
                sp.wait_ge(out_x[s], 16 * (PAIRS + 1))
                sp.wait_ge(out_T[s], 32 * (PAIRS + 1))
            sp.wait_ge(out_rs, 16 * NT)

        @block.tensor
        def _(pe):
            pe.wait_ge(w_ld, 160)
            pe.wait_ge(setup, 4)
            with pe.Fori(0, PAIRS) as it:
                def group_free(g):
                    pe.wait_ge(t_evac, it * TG + g + 1)

                def adj_transposes(s):
                    pe.wait_ge(ld_adj[s], 16 * it + 16)
                    for c in range(NT):
                        group_free(TADJ[s] + c)
                        bank = T[c % 2]
                        for t in range(NT):
                            last = nc.tensor.transpose(bank[:, t * P:t * P + P], adj_in[s][:, t, c * P:c * P + P],
                                                       ident[:])
                        last.then_inc(t_full, 1)

                def aggregate(layer, s, src, waits):
                    for w, v in waits:
                        pe.wait_ge(w, v)
                    for c in range(DC):
                        pe.wait_ge(g_evac, it * GG + AGG[layer][s] + c + 1)
                        for m in range(NT):
                            last = nc.tensor.matmul(G[c][:], src[:, m, c * P:c * P + P], adjT[s][:, m, :],
                                                    start=(m == 0), stop=(m == NT - 1))
                        last.then_inc(g_full, 1)

                def aggregate0(s):
                    aggregate(0, s, x_in[s], ((dia_done, it * 6 + s + 1), (ld_x[s], 16 * it + 16)))

                def aggregate1(s):
                    aggregate(1, s, xs[s], ((dia_done, it * 6 + 2 + s + 1), (xs_done, it * 2 + s + 1)))

                def aggregate2(s):
                    aggregate(2, s, xa[s], ((dia_done, it * 6 + 4 + s + 1), (x_done, it * 6 + 2 + s + 1)))

                def hidden(s, t):
                    if t == 0:
                        pe.wait_ge(g_evac, it * GG + AGG[0][s] + 2 + 2)
                    for q in range(2):
                        pe.wait_ge(h_evac, it * HG + 8 * s + 2 * t + q + 1)
                        for c in range(DC):
                            last = nc.tensor.matmul(HP[q][:], agg[s][:, c, t * P:t * P + P],
                                                    w1[:, c, q * 512:q * 512 + 512], start=(c == 0), stop=(c == DC - 1))
                        last.then_inc(h_full, 1)

                def hidden_transposes(s, t):
                    pe.wait_ge(y_done, it * 8 + 4 * s + t + 1)
                    for q in range(2):
                        group_free(TY[s] + 2 * t + q)
                        for k in range(4):
                            last = nc.tensor.transpose(T[q][:, k * P:k * P + P],
                                                       hb[t % 2][:, (4 * q + k) * P:(4 * q + k + 1) * P], ident[:])
                        last.then_inc(t_full, 1)

                def out_tile(layer, s, t, pairs):
                    o = 8 * layer + 4 * s + t
                    pe.wait_ge(o_evac, it * OG + o + 1)
                    for k, (lhsT, rhs) in enumerate(pairs):
                        last = nc.tensor.matmul(O[t % 2][:, 0:D], lhsT, rhs, start=(k == 0), stop=(k == len(pairs) - 1))
                    last.then_inc(o_full, 1)

                def out0(s, t):
                    pe.wait_ge(t_evac, it * TG + TY[s] + 2 * t + 2 + 2)
                    out_tile(0, s, t, [(hT[t % 2][:, k, :], w2[:, k, :]) for k in range(HC)])

                def out1(s):
                    pe.wait_ge(g_evac, it * GG + AGG[1][s] + 2 + 2)
                    for t in range(NT):
                        out_tile(1, s, t, [(agg[s][:, c, t * P:t * P + P], wg[:, c, :]) for c in range(DC)])

                def features(g, s, src):
                    for c in range(DC):
                        group_free(g + c)
                        for t in range(NT):
                            last = nc.tensor.transpose(T[c][:, t * P:t * P + P], src[:, t, c * P:c * P + P], ident[:])
                        last.then_inc(t_full, 1)

                def out2(s):
                    pe.wait_ge(t_evac, it * TG + TX[s] + 2 + 2)
                    pe.wait_ge(g_evac, it * GG + AGG[2][s] + 2 + 2)
                    for t in range(NT):
                        out_tile(2, s, t, [(xT[s][:, c, t * P:t * P + P], ws[:, c, :]) for c in range(DC)]
                                 + [(agg[s][:, c, t * P:t * P + P], ws[:, DC + c, :]) for c in range(DC)])

                def features3(s):
                    pe.wait_ge(x_done, it * 6 + 4 + s + 1)
                    features(TF[s], s, xa[s])

                adj_transposes(0)
                adj_transposes(1)
                aggregate0(0)
                for s in range(2):
                    hidden(s, 0)
                    hidden(s, 1)
                    hidden_transposes(s, 0)
                    hidden(s, 2)
                    out0(s, 0)
                    hidden_transposes(s, 1)
                    hidden(s, 3)
                    out0(s, 1)
                    hidden_transposes(s, 2)
                    out0(s, 2)
                    if s == 0:
                        aggregate0(1)
                    hidden_transposes(s, 3)
                    if s == 1:
                        aggregate1(0)
                    out0(s, 3)
                out1(0)
                aggregate1(1)
                pe.wait_ge(x_done, it * 6 + 3)
                features(TX[0], 0, xa[0])
                out1(1)
                aggregate2(0)
                out2(0)
                pe.wait_ge(x_done, it * 6 + 4)
                features(TX[1], 1, xa[1])
                aggregate2(1)
                features3(0)
                out2(1)
                features3(1)
            pe.wait_ge(rsT_full, 1)
            pe.wait_ge(t_evac, PAIRS * TG + 2)
            nc.tensor.transpose(T[0][0:NT * NB, 0:P], rs_all[:].rearrange("p t b -> p (t b)"), ident[:]).then_inc(t_full, 1)

        @block.scalar
        def _(act):
            act.sem_inc(t_evac, 2)
            act.sem_inc(g_evac, 2)
            with act.Fori(0, PAIRS) as it:
                def evac_t(g, dst, func=ACT.Copy, bank=None):
                    act.wait_ge(t_full, it * TG + g + 1)
                    nc.scalar.activation(dst, T[g % 2][:], func).then_inc(t_evac, 1)

                def evac_g(layer, s, dst):
                    for c in range(DC):
                        act.wait_ge(g_full, it * GG + AGG[layer][s] + c + 1)
                        nc.scalar.activation(dst[:, c, :], G[c][:], ACT.Copy).then_inc(g_evac, 1)

                def square(s, t):
                    act.wait_ge(h_evac, it * HG + 8 * s + 2 * t + 2 + 2)
                    act.wait_ge(r_done, it * 8 + 4 * s + t + 1)
                    act.wait_ge(sq_done, it * 8 + 4 * s + t + 1)
                    nc.scalar.activation(sqj[:], hb[t % 2][:], ACT.Square, accum_out=ss[:, t % 2:t % 2 + 1]).then_inc(sq_done, 1)

                def silu(s, t):
                    for q in range(2):
                        evac_t(TY[s] + 2 * t + q, hT[t % 2][:, 4 * q:4 * q + 4, :], ACT.Silu)

                for s in range(2):
                    if s == 0:
                        pass
                    for c in range(NT):
                        evac_t(TADJ[s] + c, adjT[s][:, c, :])
                evac_g(0, 0, agg[0])
                for s in range(2):
                    square(s, 0)
                    square(s, 1)
                    silu(s, 0)
                    square(s, 2)
                    silu(s, 1)
                    square(s, 3)
                    silu(s, 2)
                    if s == 0:
                        evac_g(0, 1, agg[1])
                    silu(s, 3)
                    if s == 1:
                        evac_g(1, 0, agg[0])
                evac_g(1, 1, agg[1])
                for c in range(DC):
                    evac_t(TX[0] + c, xT[0][:, c, :])
                evac_g(2, 0, agg[0])
                for c in range(DC):
                    evac_t(TX[1] + c, xT[1][:, c, :])
                evac_g(2, 1, agg[1])
                for s in range(2):
                    act.wait_ge(out_T[s], 32 * it + 32)
                    for c in range(DC):
                        evac_t(TF[s] + c, x3Tb[s][:, c, :])

        @block.gpsimd
        def _(pool):
            nc.gpsimd.memset(ident[:], 0.0).then_inc(setup, 1)
            pool.wait_ge(setup, 1)
            nc.gpsimd.affine_select(out=ident[:], in_=ident[:], compare_op=ALU.not_equal, fill=1.0, base=0,
                                    pattern=[[-1, P]], channel_multiplier=1).then_inc(setup, 1)
            nc.gpsimd.memset(mhalf[:], -0.5).then_inc(setup, 1)
            pool.wait_ge(setup, 3)
            pool.wait_ge(w_ld, 160)
            nc.gpsimd.tensor_scalar(eident[:], ident[:], epsc[:, 0:1], None, ALU.mult).then_inc(setup, 1)
            pool.wait_ge(setup, 4)
            for s in range(2):
                pool.sem_inc(out_x[s], 16)
                pool.sem_inc(out_T[s], 32)
            pool.sem_inc(r_done, 2)
            with pool.Fori(0, PAIRS) as it:
                n = [0]

                def plain():
                    pool.sem_inc(pool_gate, 1)

                def step(ins):
                    ins.then_inc(p_step, 1)
                    n[0] += 1
                    pool.wait_ge(p_step, it * PPER + n[0])

                def diag_eps(s):
                    pool.wait_ge(t_evac, it * TG + TADJ[s] + 4 + 2)
                    plain()
                    step(nc.gpsimd.tensor_copy(dsave[s][:], diagonal(adjT[s], NT, N)))
                    nc.gpsimd.tensor_tensor(diagonal(adjT[s], NT, N), dsave[s][:],
                                            eident[:].unsqueeze(1).to_broadcast([P, NT, P]), ALU.add).then_inc(dia_done, 1)

                def diag_one(s):
                    pool.wait_ge(g_full, it * GG + AGG[0][s] + 2)
                    nc.gpsimd.tensor_tensor(diagonal(adjT[s], NT, N), dsave[s][:],
                                            ident[:].unsqueeze(1).to_broadcast([P, NT, P]), ALU.add).then_inc(dia_done, 1)

                def diag_plain(s):
                    pool.wait_ge(g_full, it * GG + AGG[1][s] + 2)
                    plain()
                    nc.gpsimd.tensor_copy(diagonal(adjT[s], NT, N), dsave[s][:]).then_inc(dia_done, 1)

                def rms(s, t):
                    k = t % 2
                    pool.wait_ge(sq_done, it * 8 + 4 * s + t + 1 + 1)
                    plain()
                    step(nc.gpsimd.tensor_scalar(rr2[:, k:k + 1], ss[:, k:k + 1], 1.0 / H, RMS_EPS, ALU.mult, ALU.add))
                    nc.gpsimd.tensor_tensor(rr[:, k:k + 1], rr2[:, k:k + 1], mhalf[:, 0:1], ALU.pow).then_inc(r_done, 1)

                def norm(layer, s):
                    pool.wait_ge(mv_done, it * 6 + 2 * layer + s + 1)
                    plain()
                    step(nc.gpsimd.tensor_scalar(ve[:, s, :], mv[:, s, :, 1], LN_EPS, None, ALU.add))
                    nc.gpsimd.tensor_tensor(rstd[:, s, :], ve[:, s, :], mhalf[:], ALU.pow).then_inc(rstd_done, 1)

                def degree(s):
                    pool.wait_ge(rs_done, it * 2 + s + 1)
                    plain()
                    step(nc.gpsimd.tensor_scalar(rs1[:, s, :], rs[:, s, :], 1.0, None, ALU.add))
                    nc.gpsimd.tensor_tensor(dg[:, s, :], rs1[:, s, :], mhalf[:], ALU.pow).then_inc(dg_done, 1)

                diag_eps(0)
                diag_eps(1)
                degree(0)
                degree(1)
                rms(0, 0)
                rms(0, 1)
                diag_one(0)
                rms(0, 2)
                rms(0, 3)
                norm(0, 0)
                rms(1, 0)
                rms(1, 1)
                diag_one(1)
                rms(1, 2)
                rms(1, 3)
                norm(0, 1)
                diag_plain(0)
                norm(1, 0)
                diag_plain(1)
                norm(1, 1)
                norm(2, 0)
                norm(2, 1)
                assert n[0] == PPER, n[0]

        @block.vector
        def _(dve):
            dve.sem_inc(h_evac, 2)
            dve.sem_inc(o_evac, 2)
            dve.sem_inc(sq_done, 1)
            dve.wait_ge(w_ld, 160)
            with dve.Fori(0, PAIRS) as it:
                n = [0]

                def step(ins):
                    ins.then_inc(v_step, 1)
                    n[0] += 1

                def settle():
                    dve.wait_ge(v_step, it * VPER + n[0])

                def row_sums(s):
                    dve.wait_ge(ld_adj[s], 16 * it + 16)
                    nc.vector.reduce_sum(rs[:, s, :], adj_in[s][:], AX_X).then_inc(rs_done, 1)
                    dve.wait_ge(rs_done, it * 2 + s + 1)
                    step(nc.vector.tensor_copy(rs_all[:, :, 2 * it + s], rs[:, s, :]))

                def residual0(s):
                    dve.wait_ge(ld_x[s], 16 * it + 16)
                    dve.wait_ge(out_x[s], 16 * it + 16)
                    step(nc.vector.tensor_tensor(xa[s][:], x_in[s][:],
                                                 b2r[:].unsqueeze(1).to_broadcast([P, NT, D]), ALU.add))
                    settle()

                def hidden(s, t):
                    for q in range(2):
                        dve.wait_ge(h_full, it * HG + 8 * s + 2 * t + q + 1)
                        nc.vector.tensor_tensor(hb[t % 2][:, q * 512:q * 512 + 512], HP[q][:],
                                                b1r[:, q * 512:q * 512 + 512], ALU.add).then_inc(h_evac, 1)

                def rms_scale(s, t):
                    dve.wait_ge(r_done, it * 8 + 4 * s + t + 1 + 2)
                    dve.wait_ge(h_evac, it * HG + 8 * s + 2 * t + 2 + 2)
                    dve.wait_ge(sq_done, it * 8 + 4 * s + t + 2)
                    nc.vector.scalar_tensor_tensor(out=hb[t % 2][:], in0=hb[t % 2][:], scalar=rr[:, t % 2:t % 2 + 1],
                                                   in1=rmsr[:], op0=ALU.mult, op1=ALU.mult).then_inc(y_done, 1)

                def add_out(layer, s, t):
                    o = 8 * layer + 4 * s + t
                    dve.wait_ge(o_full, it * OG + o + 1)
                    if layer == 0:
                        nc.vector.tensor_tensor(xa[s][:, t, :], O[t % 2][:, 0:D], xa[s][:, t, :],
                                                ALU.add).then_inc(o_evac, 1)
                        dve.wait_ge(o_evac, it * OG + o + 1 + 2)
                    else:
                        if layer == 1:
                            nc.vector.scalar_tensor_tensor(out=tmp[:, t % 2, :], in0=O[t % 2][:, 0:D],
                                                           scalar=dg[:, s, t:t + 1], in1=bgr[:],
                                                           op0=ALU.mult, op1=ALU.add).then_inc(o_evac, 1)
                        else:
                            nc.vector.tensor_tensor(tmp[:, t % 2, :], O[t % 2][:, 0:D], bsr[:], ALU.add).then_inc(o_evac, 1)
                        dve.wait_ge(o_evac, it * OG + o + 1 + 2)
                        step(nc.vector.scalar_tensor_tensor(out=xa[s][:, t, :], in0=tmp[:, t % 2, :], scalar=0.0,
                                                            in1=xa[s][:, t, :], op0=ALU.max, op1=ALU.add))
                        settle()
                    step(nc.vector.bn_stats(stats[:, t, :], xa[s][:, t, :]))
                    settle()
                    dve.sem_inc(dve_gate, 1)
                    if t < NT - 1:
                        step(nc.vector.bn_aggr(mv[:, s, t, :], stats[:, t, :]))
                    else:
                        nc.vector.bn_aggr(mv[:, s, t, :], stats[:, t, :]).then_inc(mv_done, 1)
                        dve.wait_ge(mv_done, it * 6 + 2 * layer + s + 1)

                def normalize(layer, s):
                    dve.wait_ge(rstd_done, it * 6 + 2 * layer + s + 1)
                    for t in range(NT):
                        ins = nc.vector.tensor_scalar(xa[s][:, t, :], xa[s][:, t, :], mv[:, s, t, 0:1],
                                                      rstd[:, s, t:t + 1], ALU.subtract, ALU.mult)
                        if t < NT - 1:
                            step(ins)
                        else:
                            ins.then_inc(x_done, 1)
                    settle()
                    dve.wait_ge(x_done, it * 6 + 2 * layer + s + 1)
                    if layer == 0:
                        dve.wait_ge(dg_done, it * 2 + s + 1)
                        for t in range(NT):
                            ins = nc.vector.tensor_scalar(xs[s][:, t, :], xa[s][:, t, :], dg[:, s, t:t + 1], None, ALU.mult)
                            if t < NT - 1:
                                step(ins)
                            else:
                                ins.then_inc(xs_done, 1)

                row_sums(0)
                row_sums(1)
                for s in range(2):
                    hidden(s, 0)
                    hidden(s, 1)
                    residual0(s)
                    rms_scale(s, 0)
                    hidden(s, 2)
                    rms_scale(s, 1)
                    add_out(0, s, 0)
                    rms_scale(s, 2)
                    hidden(s, 3)
                    add_out(0, s, 1)
                    rms_scale(s, 3)
                    add_out(0, s, 2)
                    add_out(0, s, 3)
                    normalize(0, s)
                for layer in (1, 2):
                    for s in range(2):
                        for t in range(NT):
                            add_out(layer, s, t)
                        normalize(layer, s)
                assert n[0] == VPER, n[0]
            dve.wait_ge(v_step, PAIRS * VPER)
            dve.sem_inc(rsT_full, 1)
            dve.wait_ge(t_full, PAIRS * TG + 1)
            R = NT * NB
            total = T[0][0:R, 0:P]
            nc.vector.tensor_scalar(zero[0:R], total, 0.0, None, ALU.is_equal).then_inc(rsT_full, 1)
            dve.wait_ge(rsT_full, 2)
            nc.vector.tensor_tensor(safe[0:R], total, zero[0:R], ALU.add).then_inc(rsT_full, 1)
            nc.vector.tensor_scalar(nonzero[0:R], zero[0:R], -1.0, 1.0, ALU.mult, ALU.add).then_inc(rsT_full, 1)
            dve.wait_ge(rsT_full, 4)
            nc.vector.reciprocal(zero[0:R], safe[0:R]).then_inc(rsT_full, 1)
            dve.wait_ge(rsT_full, 5)
            nc.vector.tensor_tensor(rsT[0:R], zero[0:R], nonzero[0:R], ALU.mult).then_inc(rsT_full, 1)


def gated_scan(nc, x3, x3T, dinv, adj_cols, adj_pairs, adj_diag, Wx_iou, Wh_iou, Wx_co, Wh_co,
               b_ioux, b_iouh, b_coux, b_couh, out):
    NB, N, D = x3.shape
    NT, DC = N // P, D // P
    BLK = x3T.shape[4]
    SUB = 8
    NS = BLK // SUB
    SUPER = N // (2 * BLK)
    GB = 16
    NG = NB // GB
    OB = 4
    NO = NB // OB
    EB = 2
    NE = NB // EB
    NPAIR = SUB * (SUB - 1) // 2
    RD, RY = 4, 4

    def pair_at(j):
        return NB * sum(SUB - 1 - k for k in range(j))

    with ExitStack() as ctx:
        def sb(name, shape, dt=F32):
            return ctx.enter_context(nc.sbuf_tensor(name, shape, dt))

        def sem(name):
            return ctx.enter_context(nc.semaphore(name))

        state = sb("state", [P, NB, NT, D])
        hist = sb("hist", [P, DC, NG, BLK, GB])
        sums = sb("sums", [P, DC, NB, BLK])
        wx_iou = sb("wx_iou", [P, DC, 2 * D])
        wh_iou = sb("wh_iou", [P, DC, 2 * D])
        wx_co = sb("wx_co", [P, DC, D])
        wh_co = sb("wh_co", [P, DC, D])
        bias = sb("bias", [P, 6])
        bias2 = sb("bias2", [P, 6])
        ident = sb("ident2", [P, P])
        mask = [sb(f"mask{h}", [P, BLK]) for h in range(2)]
        select = sb("select", [P, GB])
        mhalf = sb("mhalf2", [P, EB])
        pairs = [sb(f"pairs{k}", [P, NPAIR * NB]) for k in range(2)]
        dv = [sb(f"dv{k}", [P, NB, SUB]) for k in range(2)]
        diag = [sb(f"diag{k}", [P, NS - 1, NG, SUB]) for k in range(2)]
        sel = sb("sel", [P, RD, NG, SUB, GB])
        newrows = sb("newrows", [P, NS - 1, NG, D])
        bgt = sb("bgt", [P, DC, NB, SUB - 2])
        PAD, STREAM = 64, 96
        xz = sb("xz", [P, DC, 4 * PAD + 3 * NB])
        at_x, at_rx = (PAD, 2 * PAD + NB), 3 * PAD + 2 * NB
        xp = [xz[:, :, a:a + NB] for a in at_x]
        rx = xz[:, :, at_rx:at_rx + NB]
        g_r = sb("g_r", [P, DC, NB])
        g_z = sb("g_z", [P, DC, NB])
        g_c = sb("g_c", [P, DC, NB])
        w_ = sb("w_", [P, DC, NB])
        u_ = sb("u_", [P, DC, NB])
        avw = sb("avw", [P, DC, NB])
        avu = sb("avu", [P, DC, NB])
        ps_ = sb("ps_", [P, DC, NB])
        st6 = sb("st6", [P, RY, EB, 6])
        mv2 = sb("mv2", [P, RY, EB, 2])
        ve2 = sb("ve2", [P, RY, EB])
        rs2 = sb("rs2", [P, RY, EB])

        colsf = [newrows[:, NS - 4:NS - 2, :, :].rearrange("p s g d -> p (s g d)"), sel[:].rearrange("p r g q b -> p (r g q b)")]
        cols = [c.rearrange("p (b t i) -> p b t i", b=OB, t=NT) for c in colsf]

        def yrow(k):
            return newrows[0:BLK, k, :, :]

        def ps(name):
            return ctx.enter_context(nc.psum_tensor(name, [P, 512], F32))

        RC = [[ps(f"RC{k}{c}") for c in range(2)] for k in range(2)]
        Z = [ps(f"Z{k}") for k in range(2)]
        X = ps("X")
        T = ps("T2")

        w_ld, setup = sem("w_ld2"), sem("setup2")
        st_ld = [sem(f"st_ld{g}") for g in range(NO)]
        hist_ld, hist_ready = sem("hist_ld"), sem("hist_ready")
        cols_ld = [sem(f"cols_ld{k}") for k in range(2)]
        sub_ld = [sem(f"sub_ld{k}") for k in range(2)]
        out_st = [sem(f"out_st{k}") for k in range(RY)]
        gate_full, gate_done = sem("gate_full"), sem("gate_done")
        rx_done, xp_done, h_done = sem("rx_done"), sem("xp_done"), sem("h_done")
        bg_done, av_done = sem("bg_done"), sem("av_done")
        rows_full, rows_done = sem("rows_full"), sem("rows_done")
        carry_full, carry_done = sem("carry_full"), sem("carry_done")
        sel_full, sel_used = sem("sel_full"), sem("sel_used")
        blk_full, blk_evac, cols_masked = sem("blk_full"), sem("blk_evac"), sem("cols_masked")
        end_full, y_done, copied = sem("end_full"), sem("y_done2"), sem("copied")
        mv_done, rstd_done, norm_done = sem("mv_done2"), sem("rstd_done2"), sem("norm_done")
        d_step, p_step = sem("d_step"), sem("p_step2")
        stored = sem("stored")
        pool_gate, dve_gate = sem("pool_gate2"), sem("dve_gate2")
        pe_gate, sp_gate = sem("pe_gate"), sem("sp_gate")

        NST = 2 * BLK
        NSU = 2 * NS
        NCA = 2 * (NS - 1)
        NSE = NS * (NS - 1)
        NBG = 2 * NS * (SUB - 2)
        DPER, PPER = 1086, 320

        block = ctx.enter_context(nc.Block())

        @block.sync
        def _(sp):
            for dst, src in ((wx_iou, Wx_iou), (wh_iou, Wh_iou), (wx_co, Wx_co), (wh_co, Wh_co)):
                sp.dma_start(dst[:], src.rearrange("(c p) n -> p c n", p=P)).then_inc(w_ld, 16)
            with nc.allow_non_contiguous_dma(reason="biases, a few hundred elements"):
                for dst, a, b in ((bias, b_ioux, b_coux), (bias2, b_iouh, b_couh)):
                    sp.dma_start(dst[:, 0:4], a.rearrange("(c p) -> p c", p=P)).then_inc(w_ld, 16)
                    sp.dma_start(dst[:, 4:6], b.rearrange("(c p) -> p c", p=P)).then_inc(w_ld, 16)
            for g in range(NO):
                for b in range(OB):
                    sp.dma_start(state[:, g * OB + b, :, :],
                                 x3[g * OB + b].rearrange("(t p) d -> p t d", p=P)).then_inc(st_ld[g], 16)
            with sp.Fori(0, SUPER) as it:
                def sub_loads(hf, s):
                    i = hf * NS + s
                    k = s % 2
                    if i >= 2:
                        sp.wait_ge(bg_done, it * NBG + (SUB - 2) * (i - 1))
                        sp.sem_inc(sp_gate, 1)
                        sp.wait_ge(xp_done, it * NST + SUB * (i - 1))
                    else:
                        sp.wait_ge(copied, it * 2 * NE + 1)
                    sp.sem_inc(sp_gate, 1)
                    u = it * NSU + i
                    sp.dma_start(pairs[k][:], adj_pairs[u].partition_broadcast(P)).then_inc(sub_ld[k], 16)
                    sp.dma_start(dv[k][:], dinv[u].partition_broadcast(P)).then_inc(sub_ld[k], 16)
                    sp.dma_start(diag[k][:], adj_diag[u]).then_inc(sub_ld[k], 16)

                for hf in range(2):
                    sp.wait_ge(h_done, (it * 2 + hf) * BLK + 1)
                    sp.sem_inc(sp_gate, 1)
                    sp.dma_start(sums[:], x3T[2 * it + hf]).then_inc(hist_ld, 16)
                    sp.wait_ge(copied, (it * 2 + hf) * NE + 1)
                    sp.sem_inc(sp_gate, 1)
                    for s in range(2):
                        sub_loads(hf, s)
                    for g in range(NO):
                        if g >= 2 or hf:
                            sp.wait_ge(blk_full, (it * 2 + hf) * NO + g - 1)
                        else:
                            sp.wait_ge(copied, it * 2 * NE + 1)
                        sp.sem_inc(sp_gate, 1)
                        sp.dma_start(cols[g % 2], adj_cols[2 * it + hf, g]).then_inc(cols_ld[g % 2], 16)
                    for s in range(2, NS):
                        sub_loads(hf, s)
            for k in range(RY):
                sp.wait_ge(out_st[k], 16 * (2 * SUPER * NE // RY))

        @block.tensor
        def _(pe):
            pe.wait_ge(w_ld, 16 * 8)
            pe.wait_ge(setup, 9)
            with pe.Fori(0, SUPER) as it:
                def block_products(hf):
                    hi = it * 2 + hf
                    pe.wait_ge(copied, hi * NE + 1)
                    for g in range(NO):
                        if hf == 0:
                            pe.wait_ge(st_ld[g], 16 * OB)
                        pe.wait_ge(cols_masked, hi * NO + g + 1)
                        pe.wait_ge(blk_evac, hi * NO + g + 1)
                        bank = RC[1][g % 2]
                        for c in range(DC):
                            for b in range(OB):
                                for t in range(NT):
                                    at = (c * OB + b) * BLK
                                    n = STREAM if at + STREAM <= 512 and (b, t) != (OB - 1, NT - 1) else BLK
                                    last = nc.tensor.matmul(bank[:, at:at + n], state[:, g * OB + b, t, c * P:c * P + P],
                                                            colsf[g % 2][:, (b * NT + t) * BLK:(b * NT + t) * BLK + n],
                                                            start=(t == 0), stop=(t == NT - 1), skip_group_check=True)
                        last.then_inc(blk_full, 1)

                def own(s, part):
                    rhs = [hist[:, k, :, s * SUB:(s + 1) * SUB, :].rearrange("p g q b -> p q g b") for k in range(DC)]
                    k2 = s % 2
                    m = (0, 1, 2, 3, 4, 5)[part]
                    if m < 2:
                        o, w, col = RC[k2][m][:, 0:256], wx_iou, m * P
                    elif m < 4:
                        o, w, col = Z[k2][:, (m - 2) * 256:(m - 1) * 256], wx_iou, m * P
                    else:
                        o, w, col = RC[k2][m - 4][:, 256:512], wx_co, (m - 4) * P
                    first_of_bank = m in (0, 1, 2)
                    for k in range(DC):
                        nc.tensor.matmul(o, w[:, k, col:col + P], rhs[k], start=(first_of_bank and k == 0),
                                         stop=False, skip_group_check=True)

                def gate(bank, at, w, col, src):
                    lead = max(0, at + STREAM - 512)
                    for k in range(DC):
                        last = nc.tensor.matmul(bank[:, at - lead:at - lead + STREAM], w[:, k, col:col + P],
                                                xz[:, k, src - lead:src - lead + STREAM], start=False,
                                                stop=(k == DC - 1), skip_group_check=True)
                    last.then_inc(gate_full, 1)

                def carry(hf, s, sp_):
                    e = (it * 2 + hf) * (NSE // 2) + s * (s - 1) // 2 + sp_
                    pe.wait_ge(sel_full, e + 1)
                    for c in range(DC):
                        for g in range(NG):
                            o = X[:, c * 256:(c + 1) * 256].rearrange("p (q b) -> p q b", b=NB)[:, :, g * GB:(g + 1) * GB]
                            last = nc.tensor.matmul(o, newrows[:, sp_, g, c * P:c * P + P], sel[:, (s * (s - 1) // 2 + sp_) % RD, g],
                                                    start=(sp_ == 0 and c == 0 and g == 0), stop=(sp_ == s - 1),
                                                    skip_group_check=True)
                    last.then_inc(sel_used, 1)

                def step(hf, s, q):
                    li = hf * BLK + s * SUB + q
                    x = at_x[q % 2]
                    k2 = s % 2
                    pe.wait_ge(xp_done, it * NST + li + 1)
                    for m in range(2):
                        gate(RC[k2][m], q * NB, wh_iou, m * P, x)
                    for m in range(2):
                        gate(Z[k2], m * 256 + q * NB, wh_iou, (2 + m) * P, x)
                    pe.wait_ge(rx_done, 2 * (it * NST + li) + 2)
                    for m in range(2):
                        gate(RC[k2][m], 256 + q * NB, wh_co, m * P, at_rx)

                for hf in range(2):
                    block_products(hf)
                    pe.wait_ge(hist_ready, 4 * (it * 2 + hf) + 4)
                    for m in range(6):
                        own(0, m)
                    for s in range(NS):
                        i = hf * NS + s
                        for q in range(SUB):
                            step(hf, s, q)
                            if s == NS - 1:
                                continue
                            if q < 6:
                                if q == 0:
                                    if s == 0:
                                        pe.wait_ge(blk_evac, (it * 2 + hf) * NO + NO + 2)
                                    else:
                                        pe.wait_ge(gate_done, 6 * (it * NST + (i - 1) * SUB + SUB))
                                own(s + 1, q)
                            if 1 <= q <= s:
                                if q == 1:
                                    pe.wait_ge(carry_done, it * NCA + hf * (NS - 1) + s)
                                carry(hf, s + 1, q - 1)
                        if s < NS - 1:
                            pe.wait_ge(h_done, it * NST + (i + 1) * SUB + 1)
                            pe.wait_ge(rows_done, it * NCA + hf * (NS - 1) + s + 1)
                            for g in range(NG):
                                for c in range(DC):
                                    last = nc.tensor.transpose(
                                        T[:, (g * DC + c) * P:(g * DC + c + 1) * P],
                                        hist[:, c, g, s * SUB:(s + 1) * SUB, :].rearrange("p q b -> p (q b)"), ident[:])
                            last.then_inc(rows_full, 1)
                            pe.wait_ge(rows_done, it * NCA + hf * (NS - 1) + s + 1 + 1)
                            carry(hf, s + 1, s)
                    pe.wait_ge(h_done, it * NST + (hf + 1) * BLK + 1)
                    for g in range(NE):
                        e = (it * 2 + hf) * NE + g
                        pe.wait_ge(copied, e if g >= 1 else e + 1)
                        pe.sem_inc(pe_gate, 1)
                        bank = (T, X)[g % 2]
                        for b in range(EB):
                            for c in range(DC):
                                last = nc.tensor.transpose(bank[0:BLK, (b * DC + c) * P:(b * DC + c + 1) * P],
                                                           hist[:, c, (g * EB + b) // GB, :, (g * EB + b) % GB], ident[:])
                        last.then_inc(end_full, 1)

        @block.scalar
        def _(act):
            act.sem_inc(blk_evac, 2)
            act.sem_inc(rows_done, 1)
            act.sem_inc(copied, 1)
            act.wait_ge(setup, 9)
            with act.Fori(0, SUPER) as it:
                for hf in range(2):
                    act.wait_ge(hist_ld, 16 * (it * 2 + hf) + 16)
                    for c in range(DC):
                        for g in range(NG):
                            nc.scalar.activation(hist[:, c, g].rearrange("p i b -> p b i"), sums[:, c, g * GB:(g + 1) * GB, :],
                                                 ACT.Copy).then_inc(hist_ready, 1)
                    act.wait_ge(hist_ready, 4 * (it * 2 + hf) + 4)
                    for g in range(NO):
                        act.wait_ge(blk_full, (it * 2 + hf) * NO + g + 1)
                        nc.scalar.activation(sums[:, :, g * OB:(g + 1) * OB, :],
                                             RC[1][g % 2][:].rearrange("p (c b i) -> p c b i", c=DC, b=OB),
                                             ACT.Copy).then_inc(blk_evac, 1)
                    for s in range(NS):
                        k2 = s % 2
                        for q in range(SUB):
                            n = it * NST + hf * BLK + s * SUB + q
                            for m in range(6):
                                act.wait_ge(gate_full, 6 * n + (4 if m == 2 else m + 1))
                                if m < 2:
                                    src, dst, f = RC[k2][m][:, q * NB:(q + 1) * NB], g_r, ACT.Sigmoid
                                elif m < 4:
                                    src, dst, f = Z[k2][:, (m - 2) * 256 + q * NB:(m - 2) * 256 + (q + 1) * NB], g_z, ACT.Sigmoid
                                else:
                                    src, dst, f = RC[k2][m - 4][:, 256 + q * NB:256 + (q + 1) * NB], g_c, ACT.Tanh
                                if m == 4 and hf + s + q >= 0:
                                    act.wait_ge(h_done, n + 1)
                                nc.scalar.activation(dst[:, m % 2, :], src, f, bias=bias[:, m:m + 1]).then_inc(gate_done, 1)
                        if s < NS - 1:
                            act.wait_ge(rows_full, it * NCA + hf * (NS - 1) + s + 1)
                            if s == 0:
                                act.wait_ge(stored, it * 2 + hf + 1)
                            nc.scalar.activation(newrows[:, s, :, :].rearrange("p g d -> p (g d)"), T[:],
                                                 ACT.Copy).then_inc(rows_done, 1)
                    for g in range(NE):
                        act.wait_ge(y_done, (it * 2 + hf) * NE + g + 1 + 1)
                        nc.scalar.activation(state[hf * BLK:(hf + 1) * BLK, g * EB:(g + 1) * EB, it, :],
                                             (T, X)[g % 2][0:BLK, :].rearrange("p (b d) -> p b d", b=EB),
                                             ACT.Copy).then_inc(copied, 1)

        @block.gpsimd
        def _(pool):
            nc.gpsimd.memset(ident[:], 0.0).then_inc(setup, 1)
            nc.gpsimd.memset(mask[0][:], 1.0).then_inc(setup, 1)
            nc.gpsimd.memset(mask[1][:], 1.0).then_inc(setup, 1)
            nc.gpsimd.memset(select[:], 0.0).then_inc(setup, 1)
            nc.gpsimd.memset(mhalf[:], -0.5).then_inc(p_step, 1)
            pool.wait_ge(setup, 4)
            nc.gpsimd.affine_select(out=ident[:], in_=ident[:], compare_op=ALU.not_equal, fill=1.0, base=0,
                                    pattern=[[-1, P]], channel_multiplier=1).then_inc(setup, 1)
            for h in range(2):
                pool.wait_ge(setup, 5 + h)
                nc.gpsimd.affine_select(out=mask[h][h * BLK:, :], in_=mask[h][h * BLK:, :], compare_op=ALU.is_ge,
                                        fill=0.0, base=0, pattern=[[-1, BLK]], channel_multiplier=1).then_inc(setup, 1)
            pool.wait_ge(setup, 7)
            for j in range(SUB):
                pool.wait_ge(p_step, 1 + j)
                nc.gpsimd.affine_select(out=select[:], in_=select[:], compare_op=ALU.not_equal, fill=1.0, base=-GB * j,
                                        pattern=[[-1, GB]], channel_multiplier=1).then_inc(p_step, 1)
            pool.sem_inc(stored, 1)
            pool.sem_inc(sel_used, RD)
            pool.wait_ge(p_step, 1 + SUB)
            with pool.Fori(0, SUPER) as it:
                n = [0]

                def step(ins):
                    ins.then_inc(p_step, 1)
                    n[0] += 1
                    pool.wait_ge(p_step, it * PPER + 1 + SUB + n[0])

                def plain():
                    pool.sem_inc(pool_gate, 1)

                def selector(hf, s, sp_):
                    e = s * (s - 1) // 2 + sp_
                    pool.wait_ge(sel_used, (it * 2 + hf) * (NSE // 2) + e + 1)
                    src = diag[s % 2][:, sp_, :, :].unsqueeze(3).to_broadcast([P, NG, SUB, GB])
                    m = select[:].unsqueeze(1).unsqueeze(1).to_broadcast([P, NG, SUB, GB])
                    nc.gpsimd.tensor_tensor(sel[:, e % RD], src, m, ALU.mult).then_inc(sel_full, 1)

                def coefficients(hf, s):
                    i = hf * NS + s
                    k = s % 2
                    pool.wait_ge(sub_ld[k], 48 * (it * NS + hf * NS // 2 + s // 2 + 1))
                    for q in range(SUB - 1):
                        c = pairs[k][:, pair_at(q):pair_at(q + 1)].rearrange("p (b m) -> p b m", b=NB)
                        ins = nc.gpsimd.tensor_tensor(c[:, :, 0], c[:, :, 0], dv[k][:, :, q + 1], ALU.mult)
                        if q < SUB - 2:
                            step(ins)
                        else:
                            ins.then_inc(av_done, 1)

                def update(hf, s, q):
                    i = hf * NS + s
                    m = SUB - 2 - q
                    pool.wait_ge(h_done, it * NST + i * SUB + q + 1 + 1)
                    c = pairs[s % 2][:, pair_at(q):pair_at(q + 1)].rearrange("p (b m) -> p b m", b=NB)[:, :, 1:]
                    for d in range(DC):
                        h = hist[:, d, :, s * SUB + q, :].unsqueeze(3).to_broadcast([P, NG, GB, m])
                        step(nc.gpsimd.tensor_tensor(bgt[:, d, :, 0:m].rearrange("p (g b) m -> p g b m", b=GB),
                                                     c.rearrange("p (g b) m -> p g b m", b=GB), h, ALU.mult))
                    to = sums[:, :, :, s * SUB + q + 2:(s + 1) * SUB]
                    nc.gpsimd.tensor_tensor(to, to, bgt[:, :, :, 0:m], ALU.add).then_inc(bg_done, 1)
                    pool.wait_ge(bg_done, it * NBG + i * (SUB - 2) + q + 1)

                for hf in range(2):
                    coefficients(hf, 0)
                    for s in range(NS):
                        if s < NS - 1:
                            coefficients(hf, s + 1)
                        for q in range(SUB):
                            if q < SUB - 2:
                                if q == 0 and s > 0:
                                    pool.wait_ge(carry_done, it * NCA + hf * (NS - 1) + s)
                                update(hf, s, q)
                            if s < NS - 1 and q <= s:
                                selector(hf, s + 1, q)
                    for g in range(NE + 1):
                        if g < NE:
                            e = (it * 2 + hf) * NE + g
                            pool.wait_ge(mv_done, e + 1)
                            plain()
                            step(nc.gpsimd.tensor_scalar(ve2[0:BLK, g % RY, :], mv2[0:BLK, g % RY, :, 1], LN_EPS, None, ALU.add))
                            nc.gpsimd.tensor_tensor(rs2[0:BLK, g % RY, :], ve2[0:BLK, g % RY, :], mhalf[0:BLK, :],
                                                    ALU.pow).then_inc(rstd_done, 1)
                        if g >= 1:
                            pool.wait_ge(norm_done, (it * 2 + hf) * NE + g)
                            plain()
                            k = (g - 1) % RY
                            pool.dma_start(out[(g - 1) * EB:g * EB, 2 * it + hf].rearrange("b i d -> i b d"),
                                           yrow(k)).then_inc(out_st[k], 16)
                    for k in range(RY):
                        pool.wait_ge(out_st[k], 16 * ((it * 2 + hf + 1) * (NE // RY)))
                        pool.sem_inc(pool_gate, 1)
                    pool.sem_inc(stored, 1)
                assert n[0] == PPER, ("PPER", n[0])

        @block.vector
        def _(dve):
            dve.sem_inc(h_done, 1)
            dve.sem_inc(y_done, 1)
            dve.wait_ge(w_ld, 16 * 8)
            dve.wait_ge(setup, 7)
            nc.vector.tensor_tensor(bias[:], bias[:], bias2[:], ALU.add).then_inc(setup, 1)
            nc.vector.memset(xz[:], 0.0).then_inc(setup, 1)
            dve.wait_ge(setup, 9)
            with dve.Fori(0, SUPER) as it:
                n = [0]

                def step(ins):
                    ins.then_inc(d_step, 1)
                    n[0] += 1

                def settle(back=0):
                    dve.wait_ge(d_step, it * DPER + n[0] - back)

                def node(hf, s, q):
                    li = hf * BLK + s * SUB + q
                    N0 = it * NST + li
                    x, xn = xp[q % 2], xp[(q + 1) % 2]
                    k = s % 2
                    last = q == SUB - 1
                    for c in range(DC):
                        dve.wait_ge(gate_done, 6 * N0 + c + 1)
                        nc.vector.tensor_tensor(rx[:, c, :], g_r[:, c, :], x[:, c, :], ALU.mult).then_inc(rx_done, 1)
                    if not last:
                        i = hf * NS + s
                        if q >= 1:
                            dve.wait_ge(bg_done, it * NBG + i * (SUB - 2) + q)
                        step(nc.vector.tensor_tensor(ps_[:], sums[:, :, :, s * SUB + q + 1],
                                                     dv[k][:, :, q + 1].unsqueeze(1).to_broadcast([P, DC, NB]), ALU.mult))
                    dve.wait_ge(h_done, N0 + 1)
                    dve.wait_ge(gate_done, 6 * N0 + 4)
                    step(nc.vector.tensor_scalar(w_[:], g_z[:], -1.0, 1.0, ALU.mult, ALU.add))
                    step(nc.vector.tensor_tensor(u_[:], g_z[:], x, ALU.mult))
                    if not last:
                        dve.wait_ge(av_done, it * NSU + hf * NS + s + 1)
                        a = pairs[k][:, pair_at(q):pair_at(q + 1)].rearrange("p (b m) -> p b m", b=NB)[:, :, 0]
                        a = a.unsqueeze(1).to_broadcast([P, DC, NB])
                        settle(1)
                        step(nc.vector.tensor_tensor(avw[:], w_[:], a, ALU.mult))
                        settle(1)
                        step(nc.vector.tensor_tensor(avu[:], u_[:], a, ALU.mult))
                        settle()
                        step(nc.vector.tensor_tensor(avu[:], ps_[:], avu[:], ALU.add))
                        dve.wait_ge(gate_done, 6 * N0 + 6)
                        step(nc.vector.tensor_tensor(avw[:], avw[:], g_c[:], ALU.mult))
                        settle()
                        nc.vector.tensor_tensor(xn, avu[:], avw[:], ALU.add).then_inc(xp_done, 1)
                    else:
                        dve.wait_ge(gate_done, 6 * N0 + 6)
                        settle()
                    step(nc.vector.tensor_tensor(w_[:], w_[:], g_c[:], ALU.mult))
                    settle()
                    nc.vector.tensor_tensor(hist[:, :, :, s * SUB + q, :], w_[:].rearrange("p c (g b) -> p c g b", b=GB),
                                            u_[:].rearrange("p c (g b) -> p c g b", b=GB), ALU.add).then_inc(h_done, 1)

                def begin(hf, s):
                    k = s % 2
                    dve.wait_ge(sub_ld[k], 48 * (it * NS + hf * NS // 2 + s // 2 + 1))
                    src = sums[:, :, :, s * SUB]
                    if s == 0:
                        dve.wait_ge(blk_evac, (it * 2 + hf) * NO + NO + 2)
                    else:
                        dve.wait_ge(sel_used, (it * 2 + hf) * (NSE // 2) + s * (s + 1) // 2 + RD)
                        carry = X[:].rearrange("p (c q b) -> p c b q", c=DC, q=SUB)
                        step(nc.vector.tensor_tensor(avw[:], sums[:, :, :, s * SUB], carry[:, :, :, 0], ALU.add))
                        settle()
                        src = avw[:]
                    ins = nc.vector.tensor_tensor(xp[0], src, dv[k][:, :, 0].unsqueeze(1).to_broadcast([P, DC, NB]), ALU.mult)
                    ins.then_inc(xp_done, 1)
                    if s > 0:
                        rest = sums[:, :, :, s * SUB + 1:(s + 1) * SUB]
                        nc.vector.tensor_tensor(rest, rest, carry[:, :, :, 1:], ALU.add).then_inc(carry_done, 1)
                        dve.wait_ge(carry_done, it * NCA + hf * (NS - 1) + s)

                def end_norm(hf, g):
                    e = (it * 2 + hf) * NE + g
                    dve.wait_ge(rstd_done, e + 1)
                    y = yrow(g % RY)
                    for b in range(EB):
                        ins = nc.vector.tensor_scalar(y[:, b, :], y[:, b, :], mv2[0:BLK, g % RY, b, 0:1],
                                                      rs2[0:BLK, g % RY, b:b + 1], ALU.subtract, ALU.mult)
                        if b < EB - 1:
                            step(ins)
                            settle()
                        else:
                            ins.then_inc(norm_done, 1)

                for hf in range(2):
                    for g in range(NO):
                        hi = it * 2 + hf
                        dve.wait_ge(cols_ld[g % 2], 16 * (hi * (NO // 2) + g // 2 + 1))
                        part = cols[g % 2][:, :, it, :]
                        nc.vector.tensor_tensor(part, part, mask[hf][:].unsqueeze(1).to_broadcast([P, OB, BLK]),
                                                ALU.mult).then_inc(cols_masked, 1)
                    for s in range(NS):
                        begin(hf, s)
                        for q in range(SUB):
                            node(hf, s, q)
                    for g in range(NE):
                        e = (it * 2 + hf) * NE + g
                        dve.wait_ge(end_full, e + 1)
                        if g >= RY:
                            dve.wait_ge(out_st[g % RY], 16 * ((it * 2 + hf) * (NE // RY) + g // RY))
                        y = yrow(g % RY)
                        nc.vector.tensor_tensor(y, (T, X)[g % 2][0:BLK, :].rearrange("p (b d) -> p b d", b=EB),
                                                state[hf * BLK:(hf + 1) * BLK, g * EB:(g + 1) * EB, it, :],
                                                ALU.add).then_inc(y_done, 1)
                        dve.wait_ge(y_done, e + 1 + 1)
                        for b in range(EB):
                            step(nc.vector.bn_stats(st6[0:BLK, g % RY, b, :], y[:, b, :]))
                        for b in range(EB):
                            settle(0 if b else 1)
                            dve.sem_inc(dve_gate, 1)
                            ins = nc.vector.bn_aggr(mv2[0:BLK, g % RY, b, :], st6[0:BLK, g % RY, b, :])
                            if b < EB - 1:
                                step(ins)
                            else:
                                ins.then_inc(mv_done, 1)
                        if g >= 1:
                            end_norm(hf, g - 1)
                    end_norm(hf, NE - 1)
                assert n[0] == DPER, ("DPER", n[0])


def build(nc, h, x3, x3T, dinv, out):
    graph_layers(nc, h["x"], h["adj"], h["L0_gnn_epsilon"], h["L0_gnn_W1"], h["L0_gnn_b1"], h["L0_gnn_rms_weight"],
                 h["L0_gnn_W2"], h["L0_gnn_b2"], h["L1_gnn_W"], h["L1_gnn_b"], h["L2_gnn_weight"], h["L2_gnn_bias"],
                 x3, x3T, dinv)
    gated_scan(nc, x3, x3T, dinv, h["adj_cols"], h["adj_pairs"], h["adj_diag"],
               h["L3_gnn_W_ioux"], h["L3_gnn_W_iouh"], h["L3_gnn_W_coux"], h["L3_gnn_W_couh"],
               h["L3_gnn_b_ioux"], h["L3_gnn_b_iouh"], h["L3_gnn_b_coux"], h["L3_gnn_b_couh"],
               out.rearrange("b (k i) d -> b k i d", i=x3T.shape[4]))


def layouts(adj):
    import numpy as np
    B, N, _ = adj.shape
    BLK, SUB, OB, GB = 64, 8, 4, 16
    K, NT, NS = N // BLK, N // P, BLK // SUB
    cols = np.ascontiguousarray(adj.reshape(B // OB, OB, NT, P, K, BLK).transpose(4, 0, 3, 1, 2, 5))
    sub = adj.reshape(B, N // SUB, SUB, N // SUB, SUB)
    pairs = []
    for u in range(N // SUB):
        a = sub[:, u, :, u, :]
        pairs.append(np.concatenate([a[:, j, j + 1:].reshape(-1) for j in range(SUB - 1)]))
    diag = np.zeros((N // SUB, GB * SUB, NS - 1, B // GB, SUB), adj.dtype)
    for u in range(N // SUB):
        k, s = divmod(u, NS)
        for e in range(s):
            a = sub[:, k * NS + e, :, u, :].reshape(B // GB, GB, SUB, SUB)
            diag[u, :, e] = a.transpose(2, 1, 0, 3).reshape(GB * SUB, B // GB, SUB)
    return {"adj_cols": cols, "adj_pairs": np.ascontiguousarray(np.stack(pairs)), "adj_diag": diag}


def kernel(**inputs):
    import numpy as np
    import concourse.bacc as bacc
    from concourse.bass_utils import run_bass_kernel_spmd as run

    nc = bacc.Bacc("TRN2", target_bir_lowering=False, num_devices=1)
    arrays, handles = {}, {}
    given = {}
    for name, a in inputs.items():
        a = np.asarray(a)
        if a.ndim == 0:
            a = a.reshape(1)
        if name in ("L1_gnn_W", "L3_gnn_W_ioux", "L3_gnn_W_iouh", "L3_gnn_W_coux", "L3_gnn_W_couh"):
            a = a.T
        given[name] = np.ascontiguousarray(a)
    given.update(layouts(given["adj"]))
    for name, a in given.items():
        arrays[f"in_{name}"] = a
        handles[name] = nc.dram_tensor(f"in_{name}", a.shape, mybir.dt.from_np(a.dtype), kind="ExternalInput").ap()
    B, N, D = given["x"].shape
    x3 = nc.dram_tensor("x3", (B, N, D), F32, kind="Internal").ap()
    x3T = nc.dram_tensor("x3T", (N // 64, P, D // P, B, 64), F32, kind="Internal").ap()
    dinv = nc.dram_tensor("dinv", (N // 8, B, 8), F32, kind="Internal").ap()
    out = nc.dram_tensor("out", (B, N, D), F32, kind="ExternalOutput").ap()
    build(nc, handles, x3, x3T, dinv, out)
    r = run(nc, [arrays], core_ids=[0])
    return r.results[0]["out"]
```

```python
from contextlib import ExitStack

import concourse.bass as bass
from concourse import mybir

ALU = mybir.AluOpType
ACT = mybir.ActivationFunctionType
F32 = mybir.dt.float32
AX_X = mybir.AxisListType.X

P = 128
LN_EPS = 1e-5
RMS_EPS = 1e-6


def diagonal(t, n, width):
    whole = t[:, :, :]
    return bass.AP(tensor=whole.tensor, offset=whole.offset,
                   ap=[whole.ap[0], [width + P, n], [1, P]])


def graph_layers(nc, x, adj, eps, W1, b1, rmsw, W2, b2, W_gcn, b_gcn, W_sage, b_sage,
                 x3, x3T, dinv):
    NB, N, D = x.shape
    H = W1.shape[1]
    NT, DC, HC = N // P, D // P, H // P
    BLK = x3T.shape[4]
    SUB = dinv.shape[2]
    PAIRS = NB // 2

    with ExitStack() as ctx:
        def sb(name, shape, dt=F32):
            return ctx.enter_context(nc.sbuf_tensor(name, shape, dt))

        def sem(name):
            return ctx.enter_context(nc.semaphore(name))

        w1 = sb("w1", [P, DC, H])
        w2 = sb("w2", [P, HC, D])
        wg = sb("wg", [P, DC, D])
        ws = sb("ws", [P, 2 * DC, D])
        b1r = sb("b1r", [P, H])
        rmsr = sb("rmsr", [P, H])
        b2r = sb("b2r", [P, D])
        bgr = sb("bgr", [P, D])
        bsr = sb("bsr", [P, D])
        epsc = sb("epsc", [P, 1])
        ident = sb("ident", [P, P])
        eident = sb("eident", [P, P])
        mhalf = sb("mhalf", [P, NT])
        rs_all = sb("rs_all", [P, NT, NB])
        rsT = sb("rsT", [P, P])
        zero = sb("zero", [P, P])
        nonzero = sb("nonzero", [P, P])
        safe = sb("safe", [P, P])

        adj_in = [sb(f"adj_in{s}", [P, NT, N]) for s in range(2)]
        x_in = [sb(f"x_in{s}", [P, NT, D]) for s in range(2)]
        adjT = [sb(f"adjT{s}", [P, NT, N]) for s in range(2)]
        dsave = [sb(f"dsave{s}", [P, NT, P]) for s in range(2)]
        xa = [sb(f"xa{s}", [P, NT, D]) for s in range(2)]
        xs = [sb(f"xs{s}", [P, NT, D]) for s in range(2)]
        agg = [sb(f"agg{s}", [P, DC, N]) for s in range(2)]
        xT = [sb(f"xT{s}", [P, DC, N]) for s in range(2)]
        x3Tb = [sb(f"x3Tb{s}", [P, DC, N]) for s in range(2)]
        hb = [sb(f"hb{k}", [P, H]) for k in range(2)]
        hT = [sb(f"hT{k}", [P, HC, P]) for k in range(2)]
        sqj = sb("sqj", [P, H])
        tmp = sb("tmp", [P, 2, D])
        ss = sb("ss", [P, 2])
        rr = sb("rr", [P, 2])
        rr2 = sb("rr2", [P, 2])
        stats = sb("stats", [P, NT, 6])
        mv = sb("mv", [P, 2, NT, 2])
        ve = sb("ve", [P, 2, NT])
        rstd = sb("rstd", [P, 2, NT])
        rs = sb("rs", [P, 2, NT])
        rs1 = sb("rs1", [P, 2, NT])
        dg = sb("dg", [P, 2, NT])

        T = [ctx.enter_context(nc.psum_tensor(f"T{k}", [P, 512], F32)) for k in range(2)]
        G = [ctx.enter_context(nc.psum_tensor(f"G{k}", [P, 512], F32)) for k in range(2)]
        HP = [ctx.enter_context(nc.psum_tensor(f"HP{k}", [P, 512], F32)) for k in range(2)]
        O = [ctx.enter_context(nc.psum_tensor(f"O{k}", [P, 512], F32)) for k in range(2)]

        w_ld = sem("w_ld")
        ld_adj = [sem(f"ld_adj{s}") for s in range(2)]
        ld_x = [sem(f"ld_x{s}") for s in range(2)]
        out_x = [sem(f"out_x{s}") for s in range(2)]
        out_T = [sem(f"out_T{s}") for s in range(2)]
        out_rs = sem("out_rs")
        setup = sem("setup")
        t_full, t_evac = sem("t_full"), sem("t_evac")
        g_full, g_evac = sem("g_full"), sem("g_evac")
        h_full, h_evac = sem("h_full"), sem("h_evac")
        o_full, o_evac = sem("o_full"), sem("o_evac")
        sq_done, r_done, y_done = sem("sq_done"), sem("r_done"), sem("y_done")
        mv_done, rstd_done, x_done, xs_done = sem("mv_done"), sem("rstd_done"), sem("x_done"), sem("xs_done")
        rs_done, dg_done = sem("rs_done"), sem("dg_done")
        dia_done = sem("dia_done")
        rsT_full = sem("rsT_full")
        pool_gate, dve_gate, sp_gate = sem("pool_gate"), sem("dve_gate"), sem("sp_gate1")
        v_step, p_step = sem("v_step"), sem("p_step")

        TG, GG, HG, OG = 32, 12, 16, 24
        AT0, AT1, Y0, Y1, XT0, XT1, XF0, XF1 = 0, 6, 10, 18, 26, 28, 30, TG + 4
        TADJ, TY, TX, TF = (AT0, AT1), (Y0, Y1), (XT0, XT1), (XF0, XF1)
        AGG = ((0, 2), (4, 6), (8, 10))
        VPER, PPER = 86, 18

        block = ctx.enter_context(nc.Block())

        @block.sync
        def _(sp):
            for dst, src in ((w1, W1.rearrange("(c p) h -> p c h", p=P)), (w2, W2.rearrange("(c p) d -> p c d", p=P)),
                             (wg, W_gcn.rearrange("(c p) d -> p c d", p=P)),
                             (ws, W_sage.rearrange("(c p) d -> p c d", p=P))):
                sp.dma_start(dst[:], src).then_inc(w_ld, 16)
            for dst, src in ((b1r, b1), (rmsr, rmsw), (b2r, b2), (bgr, b_gcn), (bsr, b_sage), (epsc, eps)):
                sp.dma_start(dst[:], src.partition_broadcast(P)).then_inc(w_ld, 16)

            def load(b, s):
                sp.dma_start(adj_in[s][:], adj[b].rearrange("(t p) m -> p t m", p=P)).then_inc(ld_adj[s], 16)
                sp.dma_start(x_in[s][:], x[b].rearrange("(t p) d -> p t d", p=P)).then_inc(ld_x[s], 16)

            def store(it, b, s):
                sp.wait_ge(x_done, it * 6 + 5 + s)
                sp.sem_inc(sp_gate, 1)
                sp.dma_start(x3[b].rearrange("(t p) d -> p t d", p=P), xa[s][:]).then_inc(out_x[s], 16)
                sp.wait_ge(t_evac, it * TG + TF[s] + 2 + 2)
                sp.sem_inc(sp_gate, 1)
                for c in range(DC):
                    sp.dma_start(x3T[:, :, c, b, :].rearrange("k p i -> p k i"),
                                 x3Tb[s][:, c, :].rearrange("p (k i) -> p k i", i=BLK)).then_inc(out_T[s], 16)

            for s in range(2):
                load(s, s)
            if PAIRS > 1:
                with sp.Fori(0, PAIRS - 1) as it:
                    for s in range(2):
                        sp.wait_ge(t_full, it * TG + TADJ[s] + 4)
                        sp.sem_inc(sp_gate, 1)
                        sp.sem_inc(sp_gate, 1)
                        sp.wait_ge(rs_done, it * 2 + s + 1)
                        sp.sem_inc(sp_gate, 1)
                        sp.wait_ge(g_full, it * GG + AGG[0][s] + 2)
                        sp.sem_inc(sp_gate, 1)
                        sp.wait_ge(o_evac, it * OG + 4 * s + 4 + 2)
                        sp.sem_inc(sp_gate, 1)
                        load(2 * it + 2 + s, s)
                    for s in range(2):
                        store(it, 2 * it + s, s)
            for s in range(2):
                store(PAIRS - 1, NB - 2 + s, s)
            sp.wait_ge(rsT_full, 6)
            for t in range(NT):
                sp.dma_start(dinv[t * P // SUB:(t + 1) * P // SUB].rearrange("u b q -> b u q"),
                             rsT[t * NB:(t + 1) * NB, :].rearrange("b (u q) -> b u q", q=SUB)).then_inc(out_rs, 16)
            for s in range(2):
                sp.wait_ge(out_x[s], 16 * (PAIRS + 1))
                sp.wait_ge(out_T[s], 32 * (PAIRS + 1))
            sp.wait_ge(out_rs, 16 * NT)

        @block.tensor
        def _(pe):
            pe.wait_ge(w_ld, 160)
            pe.wait_ge(setup, 4)

            def pair(it, first):
                def group_free(g):
                    pe.wait_ge(t_evac, it * TG + g + 1)

                def adj_transposes(s):
                    pe.wait_ge(ld_adj[s], 16 * it + 16)
                    for c in range(NT):
                        group_free(TADJ[s] + c)
                        bank = T[c % 2]
                        for t in range(NT):
                            last = nc.tensor.transpose(bank[:, t * P:t * P + P], adj_in[s][:, t, c * P:c * P + P],
                                                       ident[:])
                        last.then_inc(t_full, 1)

                def aggregate(layer, s, src, waits):
                    for w, v in waits:
                        pe.wait_ge(w, v)
                    for c in range(DC):
                        pe.wait_ge(g_evac, it * GG + AGG[layer][s] + c + 1)
                        for m in range(NT):
                            last = nc.tensor.matmul(G[c][:], src[:, m, c * P:c * P + P], adjT[s][:, m, :],
                                                    start=(m == 0), stop=(m == NT - 1))
                        last.then_inc(g_full, 1)

                def aggregate0(s):
                    aggregate(0, s, x_in[s], ((dia_done, it * 6 + s + 1), (ld_x[s], 16 * it + 16)))

                def aggregate1(s):
                    aggregate(1, s, xs[s], ((dia_done, it * 6 + 2 + s + 1), (xs_done, it * 2 + s + 1)))

                def aggregate2(s):
                    aggregate(2, s, xa[s], ((dia_done, it * 6 + 4 + s + 1), (x_done, it * 6 + 2 + s + 1)))

                def hidden(s, t):
                    if t == 0:
                        pe.wait_ge(g_evac, it * GG + AGG[0][s] + 2 + 2)
                    for q in range(2):
                        pe.wait_ge(h_evac, it * HG + 8 * s + 2 * t + q + 1)
                        for c in range(DC):
                            last = nc.tensor.matmul(HP[q][:], agg[s][:, c, t * P:t * P + P],
                                                    w1[:, c, q * 512:q * 512 + 512], start=(c == 0), stop=(c == DC - 1))
                        last.then_inc(h_full, 1)

                def hidden_transposes(s, t):
                    pe.wait_ge(y_done, it * 8 + 4 * s + t + 1)
                    for q in range(2):
                        group_free(TY[s] + 2 * t + q)
                        for k in range(4):
                            last = nc.tensor.transpose(T[q][:, k * P:k * P + P],
                                                       hb[t % 2][:, (4 * q + k) * P:(4 * q + k + 1) * P], ident[:])
                        last.then_inc(t_full, 1)

                def out_tile(layer, s, t, pairs):
                    o = 8 * layer + 4 * s + t
                    pe.wait_ge(o_evac, it * OG + o + 1)
                    for k, (lhsT, rhs) in enumerate(pairs):
                        last = nc.tensor.matmul(O[t % 2][:, 0:D], lhsT, rhs, start=(k == 0), stop=(k == len(pairs) - 1))
                    last.then_inc(o_full, 1)

                def out0(s, t):
                    pe.wait_ge(t_evac, it * TG + TY[s] + 2 * t + 2 + 2)
                    out_tile(0, s, t, [(hT[t % 2][:, k, :], w2[:, k, :]) for k in range(HC)])

                def out1(s):
                    pe.wait_ge(g_evac, it * GG + AGG[1][s] + 2 + 2)
                    for t in range(NT):
                        out_tile(1, s, t, [(agg[s][:, c, t * P:t * P + P], wg[:, c, :]) for c in range(DC)])

                def features(g, s, src):
                    for c in range(DC):
                        group_free(g + c)
                        for t in range(NT):
                            last = nc.tensor.transpose(T[c][:, t * P:t * P + P], src[:, t, c * P:c * P + P], ident[:])
                        last.then_inc(t_full, 1)

                def out2(s):
                    pe.wait_ge(t_evac, it * TG + TX[s] + 2 + 2)
                    pe.wait_ge(g_evac, it * GG + AGG[2][s] + 2 + 2)
                    for t in range(NT):
                        out_tile(2, s, t, [(xT[s][:, c, t * P:t * P + P], ws[:, c, :]) for c in range(DC)]
                                 + [(agg[s][:, c, t * P:t * P + P], ws[:, DC + c, :]) for c in range(DC)])

                def features3(s, g, done):
                    pe.wait_ge(x_done, done)
                    features(g, s, xa[s])

                if first is None:
                    pe.wait_ge(t_full, it * TG)
                    pe.sem_inc(t_full, XF1 - TG)
                    features3(1, XF1 - TG, it * 6)
                    return
                adj_transposes(0)
                if first:
                    pe.wait_ge(t_full, NT)
                    pe.sem_inc(t_full, DC)
                else:
                    features3(1, XF1 - TG, it * 6)
                adj_transposes(1)
                aggregate0(0)
                for s in range(2):
                    hidden(s, 0)
                    hidden(s, 1)
                    if s == 0:
                        aggregate0(1)
                    else:
                        out0(0, 3)
                    hidden_transposes(s, 0)
                    hidden(s, 2)
                    out0(s, 0)
                    hidden_transposes(s, 1)
                    hidden(s, 3)
                    out0(s, 1)
                    hidden_transposes(s, 2)
                    out0(s, 2)
                    hidden_transposes(s, 3)
                aggregate1(0)
                out0(1, 3)
                out1(0)
                aggregate1(1)
                out1(1)
                pe.wait_ge(x_done, it * 6 + 3)
                features(TX[0], 0, xa[0])
                aggregate2(0)
                out2(0)
                pe.wait_ge(x_done, it * 6 + 4)
                features(TX[1], 1, xa[1])
                aggregate2(1)
                features3(0, XF0, it * 6 + 5)
                out2(1)

            pair(0, True)
            with pe.Fori(1, PAIRS) as it:
                pair(it, False)
            pair(PAIRS, None)
            pe.wait_ge(rsT_full, 1)
            pe.wait_ge(t_evac, PAIRS * TG + XF1 - TG + DC + 2)
            nc.tensor.transpose(T[0][0:NT * NB, 0:P], rs_all[:].rearrange("p t b -> p (t b)"), ident[:]).then_inc(t_full, 1)

        @block.scalar
        def _(act):
            act.sem_inc(t_evac, 2)
            act.sem_inc(g_evac, 2)

            def pair(it, first):
                def evac_t(g, dst, func=ACT.Copy):
                    act.wait_ge(t_full, it * TG + g + 1)
                    nc.scalar.activation(dst, T[g % 2][:], func).then_inc(t_evac, 1)

                def evac_g(layer, s, dst):
                    for c in range(DC):
                        act.wait_ge(g_full, it * GG + AGG[layer][s] + c + 1)
                        nc.scalar.activation(dst[:, c, :], G[c][:], ACT.Copy).then_inc(g_evac, 1)

                def square(s, t):
                    act.wait_ge(h_evac, it * HG + 8 * s + 2 * t + 2 + 2)
                    act.wait_ge(r_done, it * 8 + 4 * s + t + 1)
                    act.wait_ge(sq_done, it * 8 + 4 * s + t + 1)
                    nc.scalar.activation(sqj[:], hb[t % 2][:], ACT.Square, accum_out=ss[:, t % 2:t % 2 + 1]).then_inc(sq_done, 1)

                def silu(s, t):
                    for q in range(2):
                        evac_t(TY[s] + 2 * t + q, hT[t % 2][:, 4 * q:4 * q + 4, :], ACT.Silu)

                def features3(s, g, stored_before):
                    act.wait_ge(out_T[s], stored_before)
                    for c in range(DC):
                        evac_t(g + c, x3Tb[s][:, c, :])

                if first is None:
                    act.wait_ge(t_evac, it * TG + 2)
                    act.sem_inc(t_evac, XF1 - TG)
                    features3(1, XF1 - TG, 32 * it)
                    return
                for s in range(2):
                    for c in range(NT):
                        evac_t(TADJ[s] + c, adjT[s][:, c, :])
                    if s == 0 and first:
                        act.wait_ge(t_evac, NT + 2)
                        act.sem_inc(t_evac, DC)
                    elif s == 0:
                        features3(1, XF1 - TG, 32 * it)
                evac_g(0, 0, agg[0])
                for s in range(2):
                    square(s, 0)
                    square(s, 1)
                    if s == 0:
                        evac_g(0, 1, agg[1])
                    silu(s, 0)
                    square(s, 2)
                    silu(s, 1)
                    square(s, 3)
                    silu(s, 2)
                    silu(s, 3)
                    if s == 1:
                        evac_g(1, 0, agg[0])
                evac_g(1, 1, agg[1])
                for c in range(DC):
                    evac_t(TX[0] + c, xT[0][:, c, :])
                evac_g(2, 0, agg[0])
                for c in range(DC):
                    evac_t(TX[1] + c, xT[1][:, c, :])
                evac_g(2, 1, agg[1])
                features3(0, XF0, 32 * it + 32)

            pair(0, True)
            with act.Fori(1, PAIRS) as it:
                pair(it, False)
            pair(PAIRS, None)

        @block.gpsimd
        def _(pool):
            nc.gpsimd.memset(ident[:], 0.0).then_inc(setup, 1)
            pool.wait_ge(setup, 1)
            nc.gpsimd.affine_select(out=ident[:], in_=ident[:], compare_op=ALU.not_equal, fill=1.0, base=0,
                                    pattern=[[-1, P]], channel_multiplier=1).then_inc(setup, 1)
            nc.gpsimd.memset(mhalf[:], -0.5).then_inc(setup, 1)
            pool.wait_ge(setup, 3)
            pool.wait_ge(w_ld, 160)
            nc.gpsimd.tensor_scalar(eident[:], ident[:], epsc[:, 0:1], None, ALU.mult).then_inc(setup, 1)
            pool.wait_ge(setup, 4)
            for s in range(2):
                pool.sem_inc(out_x[s], 16)
                pool.sem_inc(out_T[s], 32)
            pool.sem_inc(r_done, 2)
            with pool.Fori(0, PAIRS) as it:
                n = [0]

                def plain():
                    pool.sem_inc(pool_gate, 1)

                def step(ins):
                    ins.then_inc(p_step, 1)
                    n[0] += 1
                    pool.wait_ge(p_step, it * PPER + n[0])

                def diag_eps(s):
                    pool.wait_ge(t_evac, it * TG + TADJ[s] + 4 + 2)
                    plain()
                    step(nc.gpsimd.tensor_copy(dsave[s][:], diagonal(adjT[s], NT, N)))
                    nc.gpsimd.tensor_tensor(diagonal(adjT[s], NT, N), dsave[s][:],
                                            eident[:].unsqueeze(1).to_broadcast([P, NT, P]), ALU.add).then_inc(dia_done, 1)

                def diag_one(s):
                    pool.wait_ge(g_full, it * GG + AGG[0][s] + 2)
                    nc.gpsimd.tensor_tensor(diagonal(adjT[s], NT, N), dsave[s][:],
                                            ident[:].unsqueeze(1).to_broadcast([P, NT, P]), ALU.add).then_inc(dia_done, 1)

                def diag_plain(s):
                    pool.wait_ge(g_full, it * GG + AGG[1][s] + 2)
                    plain()
                    nc.gpsimd.tensor_copy(diagonal(adjT[s], NT, N), dsave[s][:]).then_inc(dia_done, 1)

                def rms(s, t):
                    k = t % 2
                    pool.wait_ge(sq_done, it * 8 + 4 * s + t + 1 + 1)
                    plain()
                    step(nc.gpsimd.tensor_scalar(rr2[:, k:k + 1], ss[:, k:k + 1], 1.0 / H, RMS_EPS, ALU.mult, ALU.add))
                    nc.gpsimd.tensor_tensor(rr[:, k:k + 1], rr2[:, k:k + 1], mhalf[:, 0:1], ALU.pow).then_inc(r_done, 1)

                def norm(layer, s):
                    pool.wait_ge(mv_done, it * 6 + 2 * layer + s + 1)
                    plain()
                    step(nc.gpsimd.tensor_scalar(ve[:, s, :], mv[:, s, :, 1], LN_EPS, None, ALU.add))
                    nc.gpsimd.tensor_tensor(rstd[:, s, :], ve[:, s, :], mhalf[:], ALU.pow).then_inc(rstd_done, 1)

                def degree(s):
                    pool.wait_ge(rs_done, it * 2 + s + 1)
                    plain()
                    step(nc.gpsimd.tensor_scalar(rs1[:, s, :], rs[:, s, :], 1.0, None, ALU.add))
                    nc.gpsimd.tensor_tensor(dg[:, s, :], rs1[:, s, :], mhalf[:], ALU.pow).then_inc(dg_done, 1)

                diag_eps(0)
                diag_eps(1)
                degree(0)
                degree(1)
                rms(0, 0)
                rms(0, 1)
                diag_one(0)
                rms(0, 2)
                rms(0, 3)
                rms(1, 0)
                rms(1, 1)
                norm(0, 0)
                diag_one(1)
                rms(1, 2)
                rms(1, 3)
                norm(0, 1)
                diag_plain(0)
                norm(1, 0)
                diag_plain(1)
                norm(1, 1)
                norm(2, 0)
                norm(2, 1)
                assert n[0] == PPER, n[0]

        @block.vector
        def _(dve):
            dve.sem_inc(h_evac, 2)
            dve.sem_inc(o_evac, 2)
            dve.sem_inc(sq_done, 1)
            dve.wait_ge(w_ld, 160)
            with dve.Fori(0, PAIRS) as it:
                n = [0]

                def step(ins):
                    ins.then_inc(v_step, 1)
                    n[0] += 1

                def settle():
                    dve.wait_ge(v_step, it * VPER + n[0])

                def row_sums(s):
                    dve.wait_ge(ld_adj[s], 16 * it + 16)
                    nc.vector.reduce_sum(rs[:, s, :], adj_in[s][:], AX_X).then_inc(rs_done, 1)
                    dve.wait_ge(rs_done, it * 2 + s + 1)
                    step(nc.vector.tensor_copy(rs_all[:, :, 2 * it + s], rs[:, s, :]))

                def residual0(s):
                    dve.wait_ge(ld_x[s], 16 * it + 16)
                    dve.wait_ge(out_x[s], 16 * it + 16)
                    step(nc.vector.tensor_tensor(xa[s][:], x_in[s][:],
                                                 b2r[:].unsqueeze(1).to_broadcast([P, NT, D]), ALU.add))
                    settle()

                def hidden(s, t):
                    for q in range(2):
                        dve.wait_ge(h_full, it * HG + 8 * s + 2 * t + q + 1)
                        nc.vector.tensor_tensor(hb[t % 2][:, q * 512:q * 512 + 512], HP[q][:],
                                                b1r[:, q * 512:q * 512 + 512], ALU.add).then_inc(h_evac, 1)

                def rms_scale(s, t):
                    dve.wait_ge(r_done, it * 8 + 4 * s + t + 1 + 2)
                    dve.wait_ge(h_evac, it * HG + 8 * s + 2 * t + 2 + 2)
                    dve.wait_ge(sq_done, it * 8 + 4 * s + t + 2)
                    nc.vector.scalar_tensor_tensor(out=hb[t % 2][:], in0=hb[t % 2][:], scalar=rr[:, t % 2:t % 2 + 1],
                                                   in1=rmsr[:], op0=ALU.mult, op1=ALU.mult).then_inc(y_done, 1)

                def add_out(layer, s, t):
                    o = 8 * layer + 4 * s + t
                    dve.wait_ge(o_full, it * OG + o + 1)
                    if layer == 0:
                        nc.vector.tensor_tensor(xa[s][:, t, :], O[t % 2][:, 0:D], xa[s][:, t, :],
                                                ALU.add).then_inc(o_evac, 1)
                        dve.wait_ge(o_evac, it * OG + o + 1 + 2)
                    else:
                        if layer == 1:
                            nc.vector.scalar_tensor_tensor(out=tmp[:, t % 2, :], in0=O[t % 2][:, 0:D],
                                                           scalar=dg[:, s, t:t + 1], in1=bgr[:],
                                                           op0=ALU.mult, op1=ALU.add).then_inc(o_evac, 1)
                        else:
                            nc.vector.tensor_tensor(tmp[:, t % 2, :], O[t % 2][:, 0:D], bsr[:], ALU.add).then_inc(o_evac, 1)
                        dve.wait_ge(o_evac, it * OG + o + 1 + 2)
                        step(nc.vector.scalar_tensor_tensor(out=xa[s][:, t, :], in0=tmp[:, t % 2, :], scalar=0.0,
                                                            in1=xa[s][:, t, :], op0=ALU.max, op1=ALU.add))
                        settle()
                    step(nc.vector.bn_stats(stats[:, t, :], xa[s][:, t, :]))
                    settle()
                    dve.sem_inc(dve_gate, 1)
                    if t < NT - 1:
                        step(nc.vector.bn_aggr(mv[:, s, t, :], stats[:, t, :]))
                    else:
                        nc.vector.bn_aggr(mv[:, s, t, :], stats[:, t, :]).then_inc(mv_done, 1)
                        dve.wait_ge(mv_done, it * 6 + 2 * layer + s + 1)

                def normalize(layer, s):
                    dve.wait_ge(rstd_done, it * 6 + 2 * layer + s + 1)
                    for t in range(NT):
                        ins = nc.vector.tensor_scalar(xa[s][:, t, :], xa[s][:, t, :], mv[:, s, t, 0:1],
                                                      rstd[:, s, t:t + 1], ALU.subtract, ALU.mult)
                        if t < NT - 1:
                            step(ins)
                        else:
                            ins.then_inc(x_done, 1)
                    settle()
                    dve.wait_ge(x_done, it * 6 + 2 * layer + s + 1)
                    if layer == 0:
                        dve.wait_ge(dg_done, it * 2 + s + 1)
                        for t in range(NT):
                            ins = nc.vector.tensor_scalar(xs[s][:, t, :], xa[s][:, t, :], dg[:, s, t:t + 1], None, ALU.mult)
                            if t < NT - 1:
                                step(ins)
                            else:
                                ins.then_inc(xs_done, 1)

                row_sums(0)
                row_sums(1)
                for s in range(2):
                    hidden(s, 0)
                    hidden(s, 1)
                    residual0(s)
                    rms_scale(s, 0)
                    if s == 1:
                        add_out(0, 0, 3)
                    hidden(s, 2)
                    rms_scale(s, 1)
                    if s == 1:
                        normalize(0, 0)
                    add_out(0, s, 0)
                    rms_scale(s, 2)
                    hidden(s, 3)
                    add_out(0, s, 1)
                    rms_scale(s, 3)
                    add_out(0, s, 2)
                add_out(0, 1, 3)
                normalize(0, 1)
                for layer in (1, 2):
                    for s in range(2):
                        for t in range(NT):
                            add_out(layer, s, t)
                        normalize(layer, s)
                assert n[0] == VPER, n[0]
            dve.wait_ge(v_step, PAIRS * VPER)
            dve.sem_inc(rsT_full, 1)
            dve.wait_ge(t_full, PAIRS * TG + XF1 - TG + DC + 1)
            R = NT * NB
            total = T[0][0:R, 0:P]
            nc.vector.tensor_scalar(zero[0:R], total, 0.0, None, ALU.is_equal).then_inc(rsT_full, 1)
            dve.wait_ge(rsT_full, 2)
            nc.vector.tensor_tensor(safe[0:R], total, zero[0:R], ALU.add).then_inc(rsT_full, 1)
            nc.vector.tensor_scalar(nonzero[0:R], zero[0:R], -1.0, 1.0, ALU.mult, ALU.add).then_inc(rsT_full, 1)
            dve.wait_ge(rsT_full, 4)
            nc.vector.reciprocal(zero[0:R], safe[0:R]).then_inc(rsT_full, 1)
            dve.wait_ge(rsT_full, 5)
            nc.vector.tensor_tensor(rsT[0:R], zero[0:R], nonzero[0:R], ALU.mult).then_inc(rsT_full, 1)


def gated_scan(nc, x3, x3T, dinv, adj_cols, adj_pairs, adj_diag, Wx_iou, Wh_iou, Wx_co, Wh_co,
               b_ioux, b_iouh, b_coux, b_couh, out):
    NB, N, D = x3.shape
    NT, DC = N // P, D // P
    BLK = x3T.shape[4]
    SUB = 8
    NS = BLK // SUB
    SUPER = N // (2 * BLK)
    GB = 16
    NG = NB // GB
    OB = 4
    NO = NB // OB
    EB = 2
    NE = NB // EB
    NPAIR = SUB * (SUB - 1) // 2
    RD, RY = 4, 4

    def pair_at(j):
        return NB * sum(SUB - 1 - k for k in range(j))

    with ExitStack() as ctx:
        def sb(name, shape, dt=F32):
            return ctx.enter_context(nc.sbuf_tensor(name, shape, dt))

        def sem(name):
            return ctx.enter_context(nc.semaphore(name))

        state = sb("state", [P, NB, NT, D])
        feats = sb("feats", [P, DC, NB, BLK])
        sums = sb("sums", [P, DC, NB, BLK])
        wx_iou = sb("wx_iou", [P, DC, 2 * D])
        wh_iou = sb("wh_iou", [P, DC, 2 * D])
        wx_co = sb("wx_co", [P, DC, D])
        wh_co = sb("wh_co", [P, DC, D])
        bias = sb("bias", [P, 6])
        bias2 = sb("bias2", [P, 6])
        ident = sb("ident2", [P, P])
        mask = [sb(f"mask{h}", [P, BLK]) for h in range(2)]
        select = sb("select", [P, GB])
        mhalf = sb("mhalf2", [P, EB])
        pairs = [sb(f"pairs{k}", [P, NPAIR * NB]) for k in range(2)]
        dv = [sb(f"dv{k}", [P, NB, SUB]) for k in range(2)]
        diag = [sb(f"diag{k}", [P, NS - 1, NG, SUB]) for k in range(2)]
        sel = sb("sel", [P, RD, NG, SUB, GB])
        newrows = sb("newrows", [P, NS - 1, NG, D])
        fresh = newrows[:, NS - 2, :, :].rearrange("p g d -> p (g d)").rearrange("p (c g q b) -> p c g q b", c=DC, g=NG, q=SUB)
        bgt = sb("bgt", [P, DC, NB, SUB - 2])
        PAD, STREAM = 64, 96
        xz = sb("xz", [P, DC, 4 * PAD + 3 * NB])
        at_x, at_rx = (PAD, 2 * PAD + NB), 3 * PAD + 2 * NB
        xp = [xz[:, :, a:a + NB] for a in at_x]
        rx = xz[:, :, at_rx:at_rx + NB]
        g_r = sb("g_r", [P, DC, NB])
        g_z = sb("g_z", [P, DC, NB])
        g_c = sb("g_c", [P, DC, NB])
        w_ = sb("w_", [P, DC, NB])
        u_ = sb("u_", [P, DC, NB])
        avw = sb("avw", [P, DC, NB])
        avu = sb("avu", [P, DC, NB])
        ps_ = sb("ps_", [P, DC, NB])
        st6 = sb("st6", [P, RY, EB, 6])
        mv2 = sb("mv2", [P, RY, EB, 2])
        ve2 = sb("ve2", [P, RY, EB])
        rs2 = sb("rs2", [P, RY, EB])

        colsf = [newrows[:, NS - 4:NS - 2, :, :].rearrange("p s g d -> p (s g d)"), sel[:].rearrange("p r g q b -> p (r g q b)")]
        cols = [c.rearrange("p (b t i) -> p b t i", b=OB, t=NT) for c in colsf]

        def yrow(k):
            return newrows[0:BLK, k, :, :]

        def ps(name):
            return ctx.enter_context(nc.psum_tensor(name, [P, 512], F32))

        R = [ps(f"R{k}") for k in range(2)]
        ZC = [[ps(f"ZC{k}{c}") for c in range(2)] for k in range(2)]
        X = ps("X")
        T = ps("T2")
        ends = (T, X, R[0], R[1])
        RB = len(ends)

        w_ld, setup = sem("w_ld2"), sem("setup2")
        st_ld = [sem(f"st_ld{g}") for g in range(NO)]
        feats_ld, kept = sem("feats_ld"), sem("kept")
        cols_ld = [sem(f"cols_ld{k}") for k in range(2)]
        sub_ld = [sem(f"sub_ld{k}") for k in range(2)]
        out_st = [sem(f"out_st{k}") for k in range(RY)]
        gate_full, gate_done = sem("gate_full"), sem("gate_done")
        rx_done, xp_done, h_done = sem("rx_done"), sem("xp_done"), sem("h_done")
        bg_done, av_done = sem("bg_done"), sem("av_done")
        rows_full, rows_done = sem("rows_full"), sem("rows_done")
        carry_done = sem("carry_done")
        sel_full, sel_used = sem("sel_full"), sem("sel_used")
        blk_full, blk_evac, cols_masked = sem("blk_full"), sem("blk_evac"), sem("cols_masked")
        end_full, y_done, copied = sem("end_full"), sem("y_done2"), sem("copied")
        mv_done, rstd_done, norm_done = sem("mv_done2"), sem("rstd_done2"), sem("norm_done")
        d_step, p_step = sem("d_step"), sem("p_step2")
        stored = sem("stored")
        pool_gate, dve_gate = sem("pool_gate2"), sem("dve_gate2")
        pe_gate, sp_gate = sem("pe_gate"), sem("sp_gate")

        NST = 2 * BLK
        NSU = 2 * NS
        NCA = 2 * (NS - 1)
        NSE = NS * (NS - 1)
        NPC = 6 * DC
        NBG = 2 * NS * (SUB - 2)
        DPER, PPER = 1182, 332

        block = ctx.enter_context(nc.Block())

        @block.sync
        def _(sp):
            for dst, src in ((wx_iou, Wx_iou), (wh_iou, Wh_iou), (wx_co, Wx_co), (wh_co, Wh_co)):
                sp.dma_start(dst[:], src.rearrange("(c p) n -> p c n", p=P)).then_inc(w_ld, 16)
            with nc.allow_non_contiguous_dma(reason="biases, a few hundred elements"):
                for dst, a, b in ((bias, b_ioux, b_coux), (bias2, b_iouh, b_couh)):
                    sp.dma_start(dst[:, 0:4], a.rearrange("(c p) -> p c", p=P)).then_inc(w_ld, 16)
                    sp.dma_start(dst[:, 4:6], b.rearrange("(c p) -> p c", p=P)).then_inc(w_ld, 16)
            with sp.Fori(0, SUPER) as it:
                def sub_loads(hf, s):
                    i = hf * NS + s
                    k = s % 2
                    if s >= 2:
                        sp.wait_ge(bg_done, it * NBG + (SUB - 2) * (i - 1))
                        sp.sem_inc(sp_gate, 1)
                        sp.wait_ge(xp_done, 2 * (it * NST + SUB * (i - 1)))
                        sp.sem_inc(sp_gate, 1)
                    u = it * NSU + i
                    sp.dma_start(pairs[k][:], adj_pairs[u].partition_broadcast(P)).then_inc(sub_ld[k], 16)
                    sp.dma_start(dv[k][:], dinv[u].partition_broadcast(P)).then_inc(sub_ld[k], 16)
                    sp.dma_start(diag[k][:], adj_diag[u]).then_inc(sub_ld[k], 16)

                for hf in range(2):
                    sp.wait_ge(h_done, (it * 2 + hf) * BLK + 1)
                    sp.sem_inc(sp_gate, 1)
                    for g in range(NO):
                        if g == 2:
                            sp.dma_start(feats[:], x3T[2 * it + hf]).then_inc(feats_ld, 16)
                            for s in range(2):
                                sub_loads(hf, s)
                        if g >= 2:
                            sp.wait_ge(blk_full, (it * 2 + hf) * NO + g - 1)
                            sp.sem_inc(sp_gate, 1)
                        sp.dma_start(cols[g % 2], adj_cols[2 * it + hf, g]).then_inc(cols_ld[g % 2], 16)
                    for s in range(2, NS):
                        sub_loads(hf, s)
            for k in range(RY):
                sp.wait_ge(out_st[k], 16 * (2 * SUPER * NE // RY))

        @block.tensor
        def _(pe):
            pe.wait_ge(w_ld, 16 * 8)
            pe.wait_ge(setup, 9)

            def products(hi, g):
                pe.wait_ge(cols_masked, hi * NO + g + 1)
                pe.wait_ge(blk_evac, hi * NO + g + 1)
                bank = ZC[1][g % 2]
                for c in range(DC):
                    for b in range(OB):
                        for t in range(NT):
                            at = (c * OB + b) * BLK
                            n = STREAM if at + STREAM <= 512 and (b, t) != (OB - 1, NT - 1) else BLK
                            last = nc.tensor.matmul(bank[:, at:at + n], state[:, g * OB + b, t, c * P:c * P + P],
                                                    colsf[g % 2][:, (b * NT + t) * BLK:(b * NT + t) * BLK + n],
                                                    start=(t == 0), stop=(t == NT - 1), skip_group_check=True)
                last.then_inc(blk_full, 1)

            for g in range(NO):
                pe.wait_ge(st_ld[g], 16 * OB)
                products(0, g)

            def superblock(it, final):
                def own(s, piece):
                    k2 = s % 2
                    m, k = piece // DC, piece % DC
                    if m < 2:
                        o, w, col = R[k2][:, m * 256:(m + 1) * 256], wx_iou, m * P
                    elif m < 4:
                        o, w, col = ZC[k2][m - 2][:, 0:256], wx_iou, m * P
                    else:
                        o, w, col = ZC[k2][m - 4][:, 256:512], wx_co, (m - 4) * P
                    first_of_bank = m in (0, 2, 3)
                    nc.tensor.matmul(o, w[:, k, col:col + P],
                                     feats[:, k, :, s * SUB:(s + 1) * SUB].rearrange("p b q -> p q b"),
                                     start=(first_of_bank and k == 0), stop=False, skip_group_check=True)

                def gate(bank, at, w, col, src, ks=(0, 1)):
                    lead = max(0, at + STREAM - 512)
                    for k in ks:
                        last = nc.tensor.matmul(bank[:, at - lead:at - lead + STREAM], w[:, k, col:col + P],
                                                xz[:, k, src - lead:src - lead + STREAM], start=False,
                                                stop=(k == DC - 1), skip_group_check=True)
                    if k == DC - 1:
                        last.then_inc(gate_full, 1)

                def carry(hf, s, sp_, cs=(0, 1)):
                    e = (it * 2 + hf) * (NSE // 2) + s * (s - 1) // 2 + sp_
                    if cs[0] == 0:
                        pe.wait_ge(sel_full, e + 1)
                    for c in cs:
                        for g in range(NG):
                            o = X[:, c * 256:(c + 1) * 256].rearrange("p (q b) -> p q b", b=NB)[:, :, g * GB:(g + 1) * GB]
                            last = nc.tensor.matmul(o, newrows[:, sp_, g, c * P:c * P + P], sel[:, (s * (s - 1) // 2 + sp_) % RD, g],
                                                    start=(sp_ == 0 and c == 0 and g == 0), stop=(sp_ == s - 1),
                                                    skip_group_check=True)
                    if cs[-1] == DC - 1:
                        last.then_inc(sel_used, 1)

                def step(hf, s, q, between):
                    li = hf * BLK + s * SUB + q
                    x = at_x[q % 2]
                    k2 = s % 2
                    for k in range(DC):
                        pe.wait_ge(xp_done, 2 * (it * NST + li) + k + 1)
                        for m in range(2):
                            gate(R[k2], m * 256 + q * NB, wh_iou, m * P, x, (k,))
                    for m in range(2):
                        gate(ZC[k2][m], q * NB, wh_iou, (2 + m) * P, x)
                    between()
                    for m in range(2):
                        pe.wait_ge(gate_done, 6 * (it * NST + li) + 3 + m)
                        if m:
                            pe.sem_inc(pe_gate, 1)
                            gate(ZC[k2][m], 256 + q * NB, wh_co, m * P, at_rx)
                            continue
                        for k in range(DC):
                            pe.wait_ge(rx_done, 2 * (it * NST + li) + 1 + k)
                            gate(ZC[k2][m], 256 + q * NB, wh_co, m * P, at_rx, (k,))

                def fill(hf, s, lo, hi):
                    i = hf * NS + s
                    for e in range(lo, hi):
                        if e == 0:
                            if s == 0:
                                pe.wait_ge(blk_evac, (it * 2 + hf) * NO + NO + 2)
                            else:
                                pe.wait_ge(gate_done, 6 * (it * NST + (i - 1) * SUB + SUB))
                        if e < NPC:
                            own(s + 1, e)
                            continue
                        if e == NPC:
                            pe.wait_ge(carry_done, it * NCA + hf * (NS - 1) + s)
                        carry(hf, s + 1, (e - NPC) // 2, ((e - NPC) % 2,))

                for hf in range(2):
                    pe.wait_ge(feats_ld, 16 * (it * 2 + hf) + 16)
                    pe.wait_ge(copied, (it * 2 + hf) * NE + 1)
                    for piece in range(NPC):
                        own(0, piece)
                    for s in range(NS):
                        i = hf * NS + s
                        for q in range(SUB):
                            lo, hi = (x * (NPC + 2 * s) // SUB for x in (q, q + 1))
                            if s == NS - 1:
                                lo = hi = 0
                            first = lo + (hi - lo > 2)
                            step(hf, s, q, lambda: fill(hf, s, lo, first))
                            fill(hf, s, first, hi)
                        if s < NS - 1:
                            pe.wait_ge(h_done, it * NST + (i + 1) * SUB + 1)
                            pe.wait_ge(rows_done, it * NCA + hf * (NS - 1) + s + 1)
                            for g in range(NG):
                                for c in range(DC):
                                    last = nc.tensor.transpose(
                                        T[:, (g * DC + c) * P:(g * DC + c + 1) * P],
                                        fresh[:, c, g].rearrange("p q b -> p (q b)"), ident[:])
                            last.then_inc(rows_full, 1)
                            pe.wait_ge(rows_done, it * NCA + hf * (NS - 1) + s + 1 + 1)
                            carry(hf, s + 1, s)
                    pe.wait_ge(kept, (it * 2 + hf) * NS + NS)
                    pe.sem_inc(pe_gate, 1)
                    for g in range(NE):
                        if g >= RB:
                            pe.wait_ge(copied, (it * 2 + hf) * NE + g - RB + 1 + 1)
                            pe.sem_inc(pe_gate, 1)
                        for b in range(EB):
                            for c in range(DC):
                                last = nc.tensor.transpose(ends[g % RB][0:BLK, (b * DC + c) * P:(b * DC + c + 1) * P],
                                                           sums[:, c, g * EB + b, :], ident[:])
                        last.then_inc(end_full, 1)
                        if g >= 3 and g % 2 and not (final and hf):
                            end_products(it, hf, (g - 3) // 2)
                    if not (final and hf):
                        end_products(it, hf, NO - 1)

            def end_products(it, hf, g):
                pe.wait_ge(copied, (it * 2 + hf) * NE + 2 * g + 2 + 1)
                products(it * 2 + hf + 1, g)

            with pe.Fori(0, SUPER - 1) as it:
                superblock(it, False)
            superblock(SUPER - 1, True)

        @block.scalar
        def _(act):
            def load_states(g):
                for b in range(OB):
                    act.dma_start(state[:, g * OB + b, :, :],
                                  x3[g * OB + b].rearrange("(t p) d -> p t d", p=P)).then_inc(st_ld[g], 16)

            for g in range(3):
                load_states(g)
            act.sem_inc(blk_evac, 2)
            act.sem_inc(rows_done, 1)
            act.sem_inc(copied, 1)
            act.wait_ge(setup, 9)

            def evacuate(hi, g):
                act.wait_ge(blk_full, hi * NO + g + 1)
                nc.scalar.activation(sums[:, :, g * OB:(g + 1) * OB, :],
                                     ZC[1][g % 2][:].rearrange("p (c b i) -> p c b i", c=DC, b=OB),
                                     ACT.Copy).then_inc(blk_evac, 1)

            for g in range(NO):
                evacuate(0, g)
                if g + 3 < NO:
                    load_states(g + 3)

            def superblock(it, final):
                for hf in range(2):
                    for s in range(NS):
                        k2 = s % 2
                        for q in range(SUB):
                            n = it * NST + hf * BLK + s * SUB + q
                            for m in range(6):
                                act.wait_ge(gate_full, 6 * n + (2 if m == 0 else m + 1))
                                if m < 2:
                                    src, dst, f = R[k2][:, m * 256 + q * NB:m * 256 + (q + 1) * NB], g_r, ACT.Sigmoid
                                elif m < 4:
                                    src, dst, f = ZC[k2][m - 2][:, q * NB:(q + 1) * NB], g_z, ACT.Sigmoid
                                else:
                                    src, dst, f = ZC[k2][m - 4][:, 256 + q * NB:256 + (q + 1) * NB], g_c, ACT.Tanh
                                if m == 2:
                                    act.wait_ge(h_done, n + 1)
                                nc.scalar.activation(dst[:, m % 2, :], src, f, bias=bias[:, m:m + 1]).then_inc(gate_done, 1)
                        if s >= NS - 2:
                            act.wait_ge(h_done, it * NST + hf * BLK + (s + 1) * SUB + 1)
                            nc.scalar.activation(
                                sums[:, :, :, s * SUB:(s + 1) * SUB].rearrange("p c (g b) q -> p (c g) q b", b=GB),
                                fresh.rearrange("p c g q b -> p (c g) q b"), ACT.Copy).then_inc(kept, 1)
                        if s < NS - 1:
                            if s == NS - 2:
                                act.wait_ge(kept, (it * 2 + hf) * NS + s + 1)
                            act.wait_ge(rows_full, it * NCA + hf * (NS - 1) + s + 1)
                            if s == 0:
                                act.wait_ge(stored, it * 2 + hf + 1)
                            nc.scalar.activation(newrows[:, s, :, :].rearrange("p g d -> p (g d)"), T[:],
                                                 ACT.Copy).then_inc(rows_done, 1)
                    for g in range(NE):
                        act.wait_ge(y_done, (it * 2 + hf) * NE + g + 1 + 1)
                        nc.scalar.activation(state[hf * BLK:(hf + 1) * BLK, g * EB:(g + 1) * EB, it, :],
                                             ends[g % RB][0:BLK, :].rearrange("p (b d) -> p b d", b=EB),
                                             ACT.Copy).then_inc(copied, 1)
                        if g >= 3 and g % 2 and not (final and hf):
                            evacuate(it * 2 + hf + 1, (g - 3) // 2)
                    if not (final and hf):
                        evacuate(it * 2 + hf + 1, NO - 1)

            with act.Fori(0, SUPER - 1) as it:
                superblock(it, False)
            superblock(SUPER - 1, True)

        @block.gpsimd
        def _(pool):
            nc.gpsimd.memset(ident[:], 0.0).then_inc(setup, 1)
            nc.gpsimd.memset(mask[0][:], 1.0).then_inc(setup, 1)
            nc.gpsimd.memset(mask[1][:], 1.0).then_inc(setup, 1)
            nc.gpsimd.memset(select[:], 0.0).then_inc(setup, 1)
            nc.gpsimd.memset(mhalf[:], -0.5).then_inc(p_step, 1)
            pool.wait_ge(setup, 4)
            nc.gpsimd.affine_select(out=ident[:], in_=ident[:], compare_op=ALU.not_equal, fill=1.0, base=0,
                                    pattern=[[-1, P]], channel_multiplier=1).then_inc(setup, 1)
            for h in range(2):
                pool.wait_ge(setup, 5 + h)
                nc.gpsimd.affine_select(out=mask[h][h * BLK:, :], in_=mask[h][h * BLK:, :], compare_op=ALU.is_ge,
                                        fill=0.0, base=0, pattern=[[-1, BLK]], channel_multiplier=1).then_inc(setup, 1)
            pool.wait_ge(setup, 7)
            for j in range(SUB):
                pool.wait_ge(p_step, 1 + j)
                nc.gpsimd.affine_select(out=select[:], in_=select[:], compare_op=ALU.not_equal, fill=1.0, base=-GB * j,
                                        pattern=[[-1, GB]], channel_multiplier=1).then_inc(p_step, 1)
            pool.sem_inc(stored, 1)
            pool.sem_inc(sel_used, RD)
            pool.wait_ge(p_step, 1 + SUB)
            with pool.Fori(0, SUPER) as it:
                n = [0]

                def step(ins):
                    ins.then_inc(p_step, 1)
                    n[0] += 1
                    pool.wait_ge(p_step, it * PPER + 1 + SUB + n[0])

                def plain():
                    pool.sem_inc(pool_gate, 1)

                def selector(hf, s, sp_):
                    e = s * (s - 1) // 2 + sp_
                    pool.wait_ge(sel_used, (it * 2 + hf) * (NSE // 2) + e + 1)
                    src = diag[s % 2][:, sp_, :, :].unsqueeze(3).to_broadcast([P, NG, SUB, GB])
                    m = select[:].unsqueeze(1).unsqueeze(1).to_broadcast([P, NG, SUB, GB])
                    nc.gpsimd.tensor_tensor(sel[:, e % RD], src, m, ALU.mult).then_inc(sel_full, 1)

                def coefficients(hf, s):
                    i = hf * NS + s
                    k = s % 2
                    pool.wait_ge(sub_ld[k], 48 * (it * NS + hf * NS // 2 + s // 2 + 1))
                    for q in range(SUB - 1):
                        c = pairs[k][:, pair_at(q):pair_at(q + 1)].rearrange("p (b m) -> p b m", b=NB)
                        ins = nc.gpsimd.tensor_tensor(c[:, :, 0], c[:, :, 0], dv[k][:, :, q + 1], ALU.mult)
                        if q < SUB - 2:
                            step(ins)
                        else:
                            ins.then_inc(av_done, 1)

                def update(hf, s, q):
                    i = hf * NS + s
                    m = SUB - 2 - q
                    pool.wait_ge(h_done, it * NST + i * SUB + q + 1 + 1)
                    c = pairs[s % 2][:, pair_at(q):pair_at(q + 1)].rearrange("p (b m) -> p b m", b=NB)[:, :, 1:]
                    for d in range(DC):
                        h = fresh[:, d, :, q, :].unsqueeze(3).to_broadcast([P, NG, GB, m])
                        step(nc.gpsimd.tensor_tensor(bgt[:, d, :, 0:m].rearrange("p (g b) m -> p g b m", b=GB),
                                                     c.rearrange("p (g b) m -> p g b m", b=GB), h, ALU.mult))
                    to = sums[:, :, :, s * SUB + q + 2:(s + 1) * SUB]
                    nc.gpsimd.tensor_tensor(to, to, bgt[:, :, :, 0:m], ALU.add).then_inc(bg_done, 1)
                    pool.wait_ge(bg_done, it * NBG + i * (SUB - 2) + q + 1)

                for hf in range(2):
                    coefficients(hf, 0)
                    for s in range(NS):
                        if s < NS - 1:
                            coefficients(hf, s + 1)
                        for q in range(SUB):
                            if q < SUB - 2:
                                if q == 0 and s > 0:
                                    pool.wait_ge(carry_done, it * NCA + hf * (NS - 1) + s)
                                update(hf, s, q)
                            if s < NS - 1 and q <= s:
                                selector(hf, s + 1, q)
                        if s >= NS - 2:
                            continue
                        pool.wait_ge(h_done, it * NST + hf * BLK + (s + 1) * SUB + 1)
                        for c in range(DC):
                            plain()
                            ins = nc.gpsimd.tensor_copy(
                                sums[:, c, :, s * SUB:(s + 1) * SUB].rearrange("p (g b) q -> p g q b", b=GB), fresh[:, c])
                            if c < DC - 1:
                                step(ins)
                            else:
                                ins.then_inc(kept, 1)
                    for g in range(NE + 1):
                        if g < NE:
                            e = (it * 2 + hf) * NE + g
                            pool.wait_ge(mv_done, e + 1)
                            plain()
                            step(nc.gpsimd.tensor_scalar(ve2[0:BLK, g % RY, :], mv2[0:BLK, g % RY, :, 1], LN_EPS, None, ALU.add))
                            nc.gpsimd.tensor_tensor(rs2[0:BLK, g % RY, :], ve2[0:BLK, g % RY, :], mhalf[0:BLK, :],
                                                    ALU.pow).then_inc(rstd_done, 1)
                        if g >= 1:
                            pool.wait_ge(norm_done, (it * 2 + hf) * NE + g)
                            plain()
                            k = (g - 1) % RY
                            pool.dma_start(out[(g - 1) * EB:g * EB, 2 * it + hf].rearrange("b i d -> i b d"),
                                           yrow(k)).then_inc(out_st[k], 16)
                    for k in range(RY):
                        pool.wait_ge(out_st[k], 16 * ((it * 2 + hf + 1) * (NE // RY)))
                        pool.sem_inc(pool_gate, 1)
                    pool.sem_inc(stored, 1)
                assert n[0] == PPER, ("PPER", n[0])

        @block.vector
        def _(dve):
            dve.sem_inc(h_done, 1)
            dve.sem_inc(y_done, 1)
            dve.wait_ge(w_ld, 16 * 8)
            dve.wait_ge(setup, 7)
            nc.vector.tensor_tensor(bias[:], bias[:], bias2[:], ALU.add).then_inc(setup, 1)
            nc.vector.memset(xz[:], 0.0).then_inc(setup, 1)
            dve.wait_ge(setup, 9)

            def mask_columns(it, hf, g):
                hi = it * 2 + hf
                dve.wait_ge(cols_ld[g % 2], 16 * (hi * (NO // 2) + g // 2 + 1))
                part = cols[g % 2][:, :, it, :]
                nc.vector.tensor_tensor(part, part, mask[hf][:].unsqueeze(1).to_broadcast([P, OB, BLK]),
                                        ALU.mult).then_inc(cols_masked, 1)

            for g in range(NO):
                mask_columns(0, 0, g)

            def superblock(it, final):
                n = [0]

                def step(ins):
                    ins.then_inc(d_step, 1)
                    n[0] += 1

                def settle(back=0):
                    dve.wait_ge(d_step, it * DPER + n[0] - back)

                def node(hf, s, q):
                    li = hf * BLK + s * SUB + q
                    N0 = it * NST + li
                    x, xn = xp[q % 2], xp[(q + 1) % 2]
                    k = s % 2
                    last = q == SUB - 1
                    for c in range(DC):
                        dve.wait_ge(gate_done, 6 * N0 + c + 1)
                        nc.vector.tensor_tensor(rx[:, c, :], g_r[:, c, :], x[:, c, :], ALU.mult).then_inc(rx_done, 1)
                    dve.wait_ge(h_done, N0 + 1)
                    if not last:
                        i = hf * NS + s
                        dve.wait_ge(av_done, it * NSU + i + 1)
                        a = pairs[k][:, pair_at(q):pair_at(q + 1)].rearrange("p (b m) -> p b m", b=NB)[:, :, 0]
                        a = a.unsqueeze(1).to_broadcast([P, DC, NB])

                        def others():
                            if q >= 1:
                                dve.wait_ge(bg_done, it * NBG + i * (SUB - 2) + q)
                            step(nc.vector.tensor_tensor(ps_[:], sums[:, :, :, s * SUB + q + 1],
                                                         dv[k][:, :, q + 1].unsqueeze(1).to_broadcast([P, DC, NB]), ALU.mult))

                        late = 1 <= q <= 3
                        step(nc.vector.tensor_tensor(avu[:], x, a, ALU.mult))
                        if not late:
                            others()
                        dve.wait_ge(gate_done, 6 * N0 + 4)
                        settle(0 if late else 1)
                        step(nc.vector.tensor_tensor(avu[:], g_z[:], avu[:], ALU.mult))
                        step(nc.vector.scalar_tensor_tensor(avw[:], g_z[:], 1.0, a, ALU.subtract, ALU.mult))
                        if late:
                            others()
                        settle(0 if late else 1)
                        step(nc.vector.tensor_tensor(avu[:], ps_[:], avu[:], ALU.add))
                        dve.wait_ge(gate_done, 6 * N0 + 5)
                        settle(1)
                        step(nc.vector.tensor_tensor(avw[:, 0, :], avw[:, 0, :], g_c[:, 0, :], ALU.mult))
                        step(nc.vector.tensor_tensor(u_[:], g_z[:], x, ALU.mult))
                        settle(1)
                        nc.vector.tensor_tensor(xn[:, 0, :], avu[:, 0, :], avw[:, 0, :], ALU.subtract).then_inc(xp_done, 1)
                        dve.wait_ge(gate_done, 6 * N0 + 6)
                        step(nc.vector.tensor_tensor(avw[:, 1, :], avw[:, 1, :], g_c[:, 1, :], ALU.mult))
                        step(nc.vector.scalar_tensor_tensor(w_[:], g_z[:], 1.0, g_c[:], ALU.subtract, ALU.mult))
                        settle(1)
                        nc.vector.tensor_tensor(xn[:, 1, :], avu[:, 1, :], avw[:, 1, :], ALU.subtract).then_inc(xp_done, 1)
                    else:
                        dve.wait_ge(gate_done, 6 * N0 + 4)
                        step(nc.vector.tensor_tensor(u_[:], g_z[:], x, ALU.mult))
                        dve.wait_ge(gate_done, 6 * N0 + 6)
                        step(nc.vector.scalar_tensor_tensor(w_[:], g_z[:], 1.0, g_c[:], ALU.subtract, ALU.mult))
                    settle()
                    if q == 0 and not (hf == 0 and s == 0):
                        dve.wait_ge(kept, (it * 2 + hf) * NS + s)
                    nc.vector.tensor_tensor(fresh[:, :, :, q, :], u_[:].rearrange("p c (g b) -> p c g b", b=GB),
                                            w_[:].rearrange("p c (g b) -> p c g b", b=GB), ALU.subtract).then_inc(h_done, 1)

                def begin(hf, s):
                    k = s % 2
                    dve.wait_ge(sub_ld[k], 48 * (it * NS + hf * NS // 2 + s // 2 + 1))
                    src = sums[:, :, :, s * SUB]
                    if s == 0:
                        dve.wait_ge(blk_evac, (it * 2 + hf) * NO + NO + 2)
                    else:
                        dve.wait_ge(sel_used, (it * 2 + hf) * (NSE // 2) + s * (s + 1) // 2 + RD)
                        carry = X[:].rearrange("p (c q b) -> p c b q", c=DC, q=SUB)
                        step(nc.vector.tensor_tensor(avw[:], sums[:, :, :, s * SUB], carry[:, :, :, 0], ALU.add))
                        settle()
                        src = avw[:]
                    ins = nc.vector.tensor_tensor(xp[0], src, dv[k][:, :, 0].unsqueeze(1).to_broadcast([P, DC, NB]), ALU.mult)
                    ins.then_inc(xp_done, 2)
                    if s > 0:
                        rest = sums[:, :, :, s * SUB + 1:(s + 1) * SUB]
                        nc.vector.tensor_tensor(rest, rest, carry[:, :, :, 1:], ALU.add).then_inc(carry_done, 1)
                        dve.wait_ge(carry_done, it * NCA + hf * (NS - 1) + s)

                def end_norm(hf, g):
                    e = (it * 2 + hf) * NE + g
                    dve.wait_ge(rstd_done, e + 1)
                    y = yrow(g % RY)
                    for b in range(EB):
                        ins = nc.vector.tensor_scalar(y[:, b, :], y[:, b, :], mv2[0:BLK, g % RY, b, 0:1],
                                                      rs2[0:BLK, g % RY, b:b + 1], ALU.subtract, ALU.mult)
                        if b < EB - 1:
                            step(ins)
                            settle()
                        else:
                            ins.then_inc(norm_done, 1)

                for hf in range(2):
                    for s in range(NS):
                        begin(hf, s)
                        for q in range(SUB):
                            node(hf, s, q)
                    more = not (final and hf)
                    nxt = (it, 1) if hf == 0 else (it + 1, 0)
                    for g in range(NE):
                        e = (it * 2 + hf) * NE + g
                        dve.wait_ge(end_full, e + 1)
                        if g >= RY:
                            dve.wait_ge(out_st[g % RY], 16 * ((it * 2 + hf) * (NE // RY) + g // RY))
                        y = yrow(g % RY)
                        nc.vector.tensor_tensor(y, ends[g % RB][0:BLK, :].rearrange("p (b d) -> p b d", b=EB),
                                                state[hf * BLK:(hf + 1) * BLK, g * EB:(g + 1) * EB, it, :],
                                                ALU.add).then_inc(y_done, 1)
                        dve.wait_ge(y_done, e + 1 + 1)
                        for b in range(EB):
                            step(nc.vector.bn_stats(st6[0:BLK, g % RY, b, :], y[:, b, :]))
                        for b in range(EB):
                            settle(0 if b else 1)
                            dve.sem_inc(dve_gate, 1)
                            ins = nc.vector.bn_aggr(mv2[0:BLK, g % RY, b, :], st6[0:BLK, g % RY, b, :])
                            if b < EB - 1:
                                step(ins)
                            else:
                                ins.then_inc(mv_done, 1)
                        if g >= 1:
                            end_norm(hf, g - 1)
                        if g == 1 and more:
                            mask_columns(*nxt, 0)
                        if g % 2 and more and g // 2 + 1 < NO:
                            mask_columns(*nxt, g // 2 + 1)
                    end_norm(hf, NE - 1)
                assert n[0] == DPER, ("DPER", n[0])

            with dve.Fori(0, SUPER - 1) as it:
                superblock(it, False)
            superblock(SUPER - 1, True)


def build(nc, h, x3, x3T, dinv, out):
    graph_layers(nc, h["x"], h["adj"], h["L0_gnn_epsilon"], h["L0_gnn_W1"], h["L0_gnn_b1"], h["L0_gnn_rms_weight"],
                 h["L0_gnn_W2"], h["L0_gnn_b2"], h["L1_gnn_W"], h["L1_gnn_b"], h["L2_gnn_weight"], h["L2_gnn_bias"],
                 x3, x3T, dinv)
    gated_scan(nc, x3, x3T, dinv, h["adj_cols"], h["adj_pairs"], h["adj_diag"],
               h["L3_gnn_W_ioux"], h["L3_gnn_W_iouh"], h["L3_gnn_W_coux"], h["L3_gnn_W_couh"],
               h["L3_gnn_b_ioux"], h["L3_gnn_b_iouh"], h["L3_gnn_b_coux"], h["L3_gnn_b_couh"],
               out.rearrange("b (k i) d -> b k i d", i=x3T.shape[4]))


def layouts(adj):
    import numpy as np
    B, N, _ = adj.shape
    BLK, SUB, OB, GB = 64, 8, 4, 16
    K, NT, NS = N // BLK, N // P, BLK // SUB
    cols = np.ascontiguousarray(adj.reshape(B // OB, OB, NT, P, K, BLK).transpose(4, 0, 3, 1, 2, 5))
    sub = adj.reshape(B, N // SUB, SUB, N // SUB, SUB)
    pairs = []
    for u in range(N // SUB):
        a = sub[:, u, :, u, :]
        pairs.append(np.concatenate([a[:, j, j + 1:].reshape(-1) for j in range(SUB - 1)]))
    diag = np.zeros((N // SUB, GB * SUB, NS - 1, B // GB, SUB), adj.dtype)
    for u in range(N // SUB):
        k, s = divmod(u, NS)
        for e in range(s):
            a = sub[:, k * NS + e, :, u, :].reshape(B // GB, GB, SUB, SUB)
            diag[u, :, e] = a.transpose(2, 1, 0, 3).reshape(GB * SUB, B // GB, SUB)
    return {"adj_cols": cols, "adj_pairs": np.ascontiguousarray(np.stack(pairs)), "adj_diag": diag}


def kernel(**inputs):
    import numpy as np
    import concourse.bacc as bacc
    from concourse.bass_utils import run_bass_kernel_spmd as run

    nc = bacc.Bacc("TRN2", target_bir_lowering=False, num_devices=1)
    arrays, handles = {}, {}
    given = {}
    for name, a in inputs.items():
        a = np.asarray(a)
        if a.ndim == 0:
            a = a.reshape(1)
        if name in ("L1_gnn_W", "L3_gnn_W_ioux", "L3_gnn_W_iouh", "L3_gnn_W_coux", "L3_gnn_W_couh"):
            a = a.T
        given[name] = np.ascontiguousarray(a)
    given.update(layouts(given["adj"]))
    for name, a in given.items():
        arrays[f"in_{name}"] = a
        handles[name] = nc.dram_tensor(f"in_{name}", a.shape, mybir.dt.from_np(a.dtype), kind="ExternalInput").ap()
    B, N, D = given["x"].shape
    x3 = nc.dram_tensor("x3", (B, N, D), F32, kind="Internal").ap()
    x3T = nc.dram_tensor("x3T", (N // 64, P, D // P, B, 64), F32, kind="Internal").ap()
    dinv = nc.dram_tensor("dinv", (N // 8, B, 8), F32, kind="Internal").ap()
    out = nc.dram_tensor("out", (B, N, D), F32, kind="ExternalOutput").ap()
    build(nc, handles, x3, x3T, dinv, out)
    r = run(nc, [arrays], core_ids=[0])
    return r.results[0]["out"]
```
